# Optimizing a Trainium2 kernel written in Bass

```python
import numpy as np
import jax
import jax.numpy as jnp

def _softmax(x, axis=-1):
    return jax.nn.softmax(x, axis=axis)

def _gelu(x):
    return jax.nn.gelu(x, approximate=True)

def _silu(x):
    return jax.nn.silu(x)

def _sigmoid(x):
    return jax.nn.sigmoid(x)

def _layernorm(x, axis=-1, eps=1e-05):
    m = jnp.mean(x, axis=axis, keepdims=True)
    v = jnp.var(x, axis=axis, keepdims=True)
    return (x - m) / jnp.sqrt(v + eps)

def _scatter_add(tgt, idx, src, axis=0):
    return tgt.at[idx].add(src)

def _segment_sum(src, seg, n):
    return jax.ops.segment_sum(src, seg, n)
kernel_name = 'mk_seq_preln_d1_jaxref_r8_19cc88'

def setup_inputs(seed: int=0):
    np.random.seed(seed)
    _w = jnp.asarray

    def _L0_attn_setup():
        import jax, jax.numpy as jnp
        import numpy as np
        B, T, D = (32, 256, 128)
        key = jax.random.key(seed)
        ks = jax.random.split(key, 5)
        b1 = float(np.sqrt(6.0 / (D + D)))
        b2 = float(np.sqrt(6.0 / (D + 1)))
        return {'x': jax.random.normal(ks[0], (B, T, D), dtype=jnp.float32), 'W1': jax.random.uniform(ks[1], (D, D), minval=-b1, maxval=b1, dtype=jnp.float32), 'b1_': jnp.zeros((D,), dtype=jnp.float32), 'W2': jax.random.uniform(ks[2], (1, D), minval=-b2, maxval=b2, dtype=jnp.float32), 'b2_': jnp.zeros((1,), dtype=jnp.float32)}
    _L0_attn_in = _L0_attn_setup()

    def _L0_ffn_setup():
        import jax, jax.numpy as jnp
        import numpy as np
        B, L, D = (4, 128, 128)
        E, H, K = (16, 64, 8)
        EPS = 1e-12

        def _l2norm(v, axis=-1):
            n = jnp.sqrt(jnp.sum(v * v, axis=axis, keepdims=True))
            return v / jnp.maximum(n, EPS)
        if __name__ == '__main__':
            out = reference(**setup_inputs())
            print(out.shape)
        key = jax.random.key(seed)
        ks = jax.random.split(key, 8)
        s = lambda fan_in: 1.0 / np.sqrt(fan_in)
        return {'x': jax.random.normal(ks[0], (B, L, D), jnp.float32), 'gate_w': jax.random.normal(ks[1], (E, D), jnp.float32) * s(D), 'w_gate': jax.random.normal(ks[2], (E, D, H), jnp.float32) * s(D), 'w_up': jax.random.normal(ks[3], (E, D, H), jnp.float32) * s(D), 'w_down': jax.random.normal(ks[4], (E, H, D), jnp.float32) * s(H), 'sw_gate': jax.random.normal(ks[5], (D, H), jnp.float32) * s(D), 'sw_up': jax.random.normal(ks[6], (D, H), jnp.float32) * s(D), 'sw_down': jax.random.normal(ks[7], (H, D), jnp.float32) * s(H)}
    _L0_ffn_in = _L0_ffn_setup()
    _d = {'L0_attn_x': _L0_attn_in['x'], 'L0_attn_W1': _L0_attn_in['W1'], 'L0_attn_b1_': _L0_attn_in['b1_'], 'L0_attn_W2': _L0_attn_in['W2'], 'L0_attn_b2_': _L0_attn_in['b2_'], 'L0_ffn_gate_w': _L0_ffn_in['gate_w'], 'L0_ffn_w_gate': _L0_ffn_in['w_gate'], 'L0_ffn_w_up': _L0_ffn_in['w_up'], 'L0_ffn_w_down': _L0_ffn_in['w_down'], 'L0_ffn_sw_gate': _L0_ffn_in['sw_gate'], 'L0_ffn_sw_up': _L0_ffn_in['sw_up'], 'L0_ffn_sw_down': _L0_ffn_in['sw_down']}
    _x0 = _d['L0_attn_x']
    _d['L0_attn_x'] = jax.random.normal(jax.random.fold_in(jax.random.key(seed), 1), (4, 1024, 128), dtype=_x0.dtype)
    del _x0
    return _d

def reference(L0_attn_x, L0_attn_W1, L0_attn_b1_, L0_attn_W2, L0_attn_b2_, L0_ffn_gate_w, L0_ffn_w_gate, L0_ffn_w_up, L0_ffn_w_down, L0_ffn_sw_gate, L0_ffn_sw_up, L0_ffn_sw_down):

    def _L0_attn_ref(x, W1, b1_, W2, b2_):
        import jax, jax.numpy as jnp
        import numpy as np
        B, T, D = (32, 256, 128)
        h = jnp.tanh(jnp.einsum('btd,ed->bte', x, W1) + b1_)
        s = jnp.einsum('bte,oe->bto', h, W2) + b2_
        m = jnp.max(s, axis=1, keepdims=True)
        e = jnp.exp(s - m)
        num = jnp.cumsum(e * x, axis=1)
        den = jnp.cumsum(e, axis=1)
        context = num / den
        return context

    def _L0_ffn_ref(x, gate_w, w_gate, w_up, w_down, sw_gate, sw_up, sw_down):
        import jax, jax.numpy as jnp
        import numpy as np
        B, L, D = (4, 128, 128)
        E, H, K = (16, 64, 8)
        EPS = 1e-12

        def _l2norm(v, axis=-1):
            n = jnp.sqrt(jnp.sum(v * v, axis=axis, keepdims=True))
            return v / jnp.maximum(n, EPS)
        if __name__ == '__main__':
            out = reference(**setup_inputs())
            print(out.shape)
        b, l, d = x.shape
        xf = x.reshape(-1, d)
        logits = _l2norm(xf) @ _l2norm(gate_w).T
        scores = jax.nn.sigmoid(logits)
        topk_scores, topk_idx = jax.lax.top_k(scores, K)
        topk_w = topk_scores / jnp.sum(topk_scores, axis=-1, keepdims=True)
        combine = jnp.sum(jax.nn.one_hot(topk_idx, E, dtype=xf.dtype) * topk_w[..., None], axis=1)
        g = jnp.einsum('nd,edh->neh', xf, w_gate)
        u = jnp.einsum('nd,edh->neh', xf, w_up)
        y = jnp.einsum('neh,ehd->ned', jax.nn.silu(g) * u, w_down)
        routed = jnp.einsum('ned,ne->nd', y, combine)
        shared = jax.nn.silu(xf @ sw_gate) * (xf @ sw_up) @ sw_down
        return (routed + shared).reshape(b, l, d)
    x = L0_attn_x
    x = x + _L0_attn_ref(_layernorm(x, axis=-1), L0_attn_W1, L0_attn_b1_, L0_attn_W2, L0_attn_b2_)
    x = x + _L0_ffn_ref(_layernorm(x, axis=-1), L0_ffn_gate_w, L0_ffn_w_gate, L0_ffn_w_up, L0_ffn_w_down, L0_ffn_sw_gate, L0_ffn_sw_up, L0_ffn_sw_down)
    return x

_drawn_inputs = setup_inputs


def setup_inputs(seed=0):
    import zlib

    import numpy as np

    out = dict(_drawn_inputs(seed))
    spreads = {'L0_attn_b1_': (0.0, 0.717)}
    factors = {}
    for name, (base, spread) in spreads.items():
        noise = np.random.default_rng([zlib.crc32(name.encode()), seed]).standard_normal(out[name].shape)
        drawn = base * np.exp(spread * noise) if base else spread * noise
        out[name] = jnp.asarray(drawn.astype(out[name].dtype))
    for name, factor in factors.items():
        out[name] = (out[name] * factor).astype(out[name].dtype)
    return out
```

```python
import concourse.bass as bass
from concourse import mybir
from contextlib import ExitStack

B, T, D = 4, 1024, 128
E, H, K = 16, 64, 8
P = 128
HALF = T // 2
TILES = HALF // P
PAIRS = E // 2
CHUNKS = 1 + PAIRS
STEPS = 2 * CHUNKS
LAG = 2
EPS = 1e-5
NORM_EPS = 1e-12
GU = 2 * H + 2 * E * H
GATE = slice(2 * H, 2 * H + E * H)
UP = slice(2 * H + E * H, GU)

STAGES = {
    0: [("route", 0, 0), ("weigh", 0, 1)],
    1: [("scan", 0, 1), ("collect", -1, 1)],
    2: [("out", -1, 1)],
    3: [("attend", 0, 1), ("stats1", 1, 0)],
    4: [("norm2", 0, 1), ("norm1", 1, 0)],
    5: [("spread2", 0, 1), ("spread1", 1, 0), ("stats1", 1, 1)],
    6: [("logits", 0, 1), ("hidden", 1, 0), ("norm1", 1, 1)],
    7: [("score", 1, 0), ("spread1", 1, 1)],
    8: [("gates", 0, 1), ("hidden", 1, 1)],
    9: [("route", 0, 1), ("score", 1, 1)],
    10: [("softmax", 1, 0), ("collect", 0, 0)],
    11: [("out", 0, 0), ("sums", 1, 0), ("weigh", 1, 0)],
    12: [("scan", 1, 0), ("denominator", 1, 0)],
    13: [("attend", 1, 0)],
    14: [("norm2", 1, 0)],
    15: [("spread2", 1, 0)],
    16: [("logits", 1, 0)],
    17: [("gates", 1, 0)],
}
FIRST_STAGES = [
    ("small_weights", 0), ("stats1", 0), ("norm1", 0), ("stats1", 1), ("norm1", 1),
    ("spread1", 0), ("hidden", 0), ("score", 0), ("spread1", 1), ("shared_weights", 0), ("hidden", 1),
    ("score", 1), ("softmax", 0), ("gate_weights", 0), ("sums", 0), ("weigh", 0), ("scan", 0), ("denominator", 0),
    ("attend", 0), ("norm2", 0), ("up_weights", 0), ("spread2", 0), ("logits", 0), ("gates", 0), ("down_weights", 0),
]
HEAD = 3


def attention_moe_kernel(nc: bass.Bass, x, w1, b1, w2, b2, gate_w, w_gate, w_up, w_down,
                         sw_gate, sw_up, sw_down, identity, pair_select, upto, out):
    f32 = mybir.dt.float32
    f32r = mybir.dt.float32r
    ALU = mybir.AluOpType
    ACT = mybir.ActivationFunctionType
    AX = mybir.AxisListType

    ctx = ExitStack()
    with ctx:
        def sb(name, shape, dt=f32):
            return ctx.enter_context(nc.sbuf_tensor(name, shape, dt))

        def pb(name):
            return ctx.enter_context(nc.psum_tensor(name, [P, HALF], f32))

        def sem(name):
            return ctx.enter_context(nc.semaphore(name))

        def word(ap):
            return ap.bitcast(f32)

        ident = sb("ident", [P, P])
        upto_sb = sb("upto_sb", [P, P])
        ones = sb("ones", [P, P])
        select_f = sb("select_f", [2 * E, PAIRS * P])
        select = sb("select", [2 * E, PAIRS * P], f32r)
        w1_sb = sb("w1_sb", [P, D])
        w1t = sb("w1t", [P, P])
        w1t_hi, w1t_lo = sb("w1t_hi", [P, P], f32r), sb("w1t_lo", [P, P], f32r)
        w2_col = sb("w2_col", [P, 1])
        b1_col = sb("b1_col", [P, 1])
        b2_sb = sb("b2_sb", [1, 1])
        gw_sb = sb("gw_sb", [E, D])
        gw_sq = sb("gw_sq", [E, D])
        gw_n2 = sb("gw_n2", [E, 1])
        gw_inv = sb("gw_inv", [E, 1])
        gw_unit = sb("gw_unit", [E, D])
        gwt = sb("gwt", [P, P])
        gwt_hi, gwt_lo = sb("gwt_hi", [P, P], f32r), sb("gwt_lo", [P, P], f32r)
        gu_sb = sb("gu_sb", [P, GU])
        gu_hi, gu_lo = sb("gu_hi", [P, GU], f32r), sb("gu_lo", [P, GU], f32r)
        dn_sb = sb("dn_sb", [P, CHUNKS * D])
        dn_hi, dn_lo = sb("dn_hi", [P, CHUNKS * D], f32r), sb("dn_lo", [P, CHUNKS * D], f32r)
        euler = sb("euler", [P, 2 * TILES])
        minus_half = sb("minus_half", [P, TILES])
        zeros = sb("zeros", [P, HALF])

        def pair(name, shape, dt=f32):
            return [sb(f"{name}{h}", shape, dt) for h in range(2)]

        x_in = pair("x_in", [P, TILES, D])
        x_res = pair("x_res", [P, TILES, D])
        xn = pair("xn", [P, TILES, D])
        bn1, bn2 = pair("bn1_", [P, TILES, 6]), pair("bn2_", [P, TILES, 6])
        mv1, mv2 = pair("mv1_", [P, TILES, 2]), pair("mv2_", [P, TILES, 2])
        var_eps1, var_eps2 = pair("var_eps1_", [P, TILES]), pair("var_eps2_", [P, TILES])
        neg_mean1, neg_mean2 = pair("neg_mean1_", [P, TILES]), pair("neg_mean2_", [P, TILES])
        rstd1, rstd2 = pair("rstd1_", [P, TILES]), pair("rstd2_", [P, TILES])
        shift1, shift2 = pair("shift1_", [P, TILES]), pair("shift2_", [P, TILES])
        var512 = pair("var512_", [P, TILES])
        xf_norm = pair("xf_norm", [P, TILES])
        xf_norm2 = pair("xf_norm2_", [P, TILES])
        xf_norm3 = pair("xf_norm3_", [P, TILES])
        half_inv = pair("half_inv", [P, TILES])
        xnt_hi, xnt_lo = sb("xnt_hi", [P, HALF], f32r), sb("xnt_lo", [P, HALF], f32r)
        hid = sb("hid", [P, HALF])
        score_row = pair("score_row", [1, HALF])
        score = sb("score", [P, 2 * TILES])
        top = sb("top", [P, 1])
        own_score = sb("own_score", [P, 2 * TILES])
        top_all = sb("top_all", [P, 1])
        below = sb("below", [P, 2 * TILES])
        weight = sb("weight", [P, 2 * TILES])
        tile_sums = sb("tile_sums", [P, 2 * TILES + 1])
        inv_den = sb("inv_den", [P, 2 * TILES])
        xw = sb("xw", [P, TILES, D])
        num_t = pair("num_t", [P, HALF])
        xf = sb("xf", [P, TILES, D])
        xft_hi, xft_lo = pair("xft_hi", [P, HALF], f32r), pair("xft_lo", [P, HALF], f32r)

        logit_t = sb("logit_t", [E, HALF])
        tanh_half = sb("tanh_half", [P, TILES, E])
        gate = sb("gate", [P, TILES, E])
        best = sb("best", [P, TILES, K])
        struck = sb("struck", [P, TILES, E])
        chosen = sb("chosen", [P, TILES, E])
        best_sum = sb("best_sum", [P, TILES])
        inv_best = sb("inv_best", [P, TILES])
        comb = sb("comb", [P, TILES, E])
        comb_hl = sb("comb_hl", [P, TILES, 2 * E], f32r)
        comb_t = pair("comb_t", [2 * E, HALF], f32r)

        silu = [sb(f"silu{i}", [P, HALF]) for i in range(2)]
        prod = [sb(f"prod{i}", [P, HALF]) for i in range(2)]
        hfull = [sb(f"hfull{i}", [P, HALF]) for i in range(2)]
        h_hi = [sb(f"h_hi{i}", [P, HALF], f32r) for i in range(3)]
        h_lo = [sb(f"h_lo{i}", [P, HALF], f32r) for i in range(3)]
        h_shared = sb("h_shared", [P, HALF], f32r)
        y_t = sb("y_t", [P, HALF])
        result = pair("result", [P, TILES, D])

        ps_gate = [pb("ps_gate0"), pb("ps_gate1")]
        ps_up = [pb("ps_up0"), pb("ps_up1")]
        ps_comb = pb("ps_comb")
        ps_y = pb("ps_y")
        ps_a = pb("ps_a")
        ps_b = pb("ps_b")

        BANK = {}
        for stage, first, second in (
                ("spread1", ps_b, ps_a), ("hidden", ps_b, ps_a), ("score", ps_b, ps_a), ("softmax", ps_a, None),
                ("denominator", ps_b, None), ("scan", ps_a, ps_b), ("attend", ps_a, ps_b), ("spread2", ps_b, ps_a),
                ("logits", ps_a, ps_a), ("gates", ps_a, ps_b), ("route", ps_a, ps_b), ("out", ps_b, ps_a)):
            BANK[stage, 0], BANK[stage, 1] = first, second

        names = """ident_in small_in gwt_in select_in shared_in gate_in up_in down_in
            consts_set w1t_ps w1t_split gw_squared gw_scaled gw_unit_set gwt_ps gwt_split gwt_zeroed
            select_set shared_hi shared_lo gu_hi_set gu_lo_set dn_hi_set dn_lo_set
            stats1_dve stats1_set scale1_pool scale1_set xn_set xnt_ps xnt_hi_set xnt_lo_set
            hid_ps hid_set score_ps score_row_set score_cols_ps score_dve top_set weight_pool
            weight_set sums_set den_ps inv_den_set xw_set xwt_ps num_set num_ps attended
            stats2_dve stats2_set scale2_pool scale2_set half_inv_set xf_set xft_ps xft_hi_set
            xft_lo_set logit_ps logit_set logit_cols_ps tanh_set route_dve comb_set comb_ps
            comb_t_set gate_ready up_ready comb_ready silu_set prod_set hfull_set h_hi_set
            h_lo_set shared_lo_set down_done y_set out_ps result_set""".split()
        s = {n: sem(n) for n in names}
        x_in_loaded = [sem("x_in_loaded0"), sem("x_in_loaded1")]
        x_res_loaded = [sem("x_res_loaded0"), sem("x_res_loaded1")]
        stored = [sem("stored0"), sem("stored1")]

        block = ctx.enter_context(nc.Block())

        def half_no(b, h):
            return 2 * b + h

        def chunk_no(b, h, i):
            return STEPS * b + CHUNKS * h + i

        def wait(eng, name, value):
            if not isinstance(value, int) or value > 0:
                eng.wait_ge(s[name], value)

        def run(step, stages, eng, stages_first=False):
            for name, h in FIRST_STAGES:
                if name in stages:
                    stages[name](0, h)

            def steps(b, first, last, before=True, after=True):
                for n in range(first, last):
                    if not stages_first:
                        step(b, n // CHUNKS, n % CHUNKS)
                    for name, ahead, h in STAGES[n]:
                        if name in stages and (ahead != -1 or before) and (ahead != 1 or after):
                            stages[name](b + ahead, h)
                    if stages_first:
                        step(b, n // CHUNKS, n % CHUNKS)

            steps(0, 0, HEAD, before=False)
            with eng.Fori(0, B - 1) as b:
                steps(b, HEAD, STEPS)
                steps(b + 1, 0, HEAD)
            steps(B - 1, HEAD, STEPS, after=False)

        def tile(t):
            return slice(t * P, (t + 1) * P)

        @block.sync
        def _(sp):
            def rows(src, b, h):
                return src[b, h * HALF:(h + 1) * HALF, :].rearrange("(t p) d -> p t d", p=P)

            sp.dma_start(x_in[0][:], rows(x, 0, 0)).then_inc(x_in_loaded[0], 16)
            sp.dma_start(x_in[1][:], rows(x, 0, 1)).then_inc(x_in_loaded[1], 16)
            sp.dma_start(gu_sb[:, 2 * H:2 * H + E * H].rearrange("d (e h) -> d e h", e=E),
                         w_gate.rearrange("e d h -> d e h")).then_inc(s["gate_in"], 16)
            sp.dma_start(gu_sb[:, 2 * H + E * H:GU].rearrange("d (e h) -> d e h", e=E),
                         w_up.rearrange("e d h -> d e h")).then_inc(s["up_in"], 16)
            sp.dma_start(x_res[0][:], rows(x, 0, 0)).then_inc(x_res_loaded[0], 16)
            sp.dma_start(x_res[1][:], rows(x, 0, 1)).then_inc(x_res_loaded[1], 16)
            sp.dma_start(dn_sb[:, D:].rearrange("p (c d) -> p c d", c=PAIRS),
                         w_down.rearrange("(c e) h d -> (e h) c d", c=PAIRS)).then_inc(s["down_in"], 16)
            sp.dma_start(dn_sb[0:H, 0:D], sw_down).then_inc(s["down_in"], 16)
            sp.dma_start(dn_sb[H:P, 0:D], sw_down).then_inc(s["down_in"], 16)

            def store_and_reload(b, h, more):
                sp.wait_ge(s["result_set"], half_no(b, h) + 1)
                sp.dma_start(rows(out, b, h), result[h][:]).then_inc(stored[h], 16)
                if more:
                    sp.dma_start(x_res[h][:], rows(x, b + 1, h)).then_inc(x_res_loaded[h], 16)

            with sp.Fori(0, B - 1) as b:
                for h in range(2):
                    sp.wait_ge(s["xn_set"], half_no(b, h) + 1)
                    sp.dma_start(x_in[h][:], rows(x, b + 1, h)).then_inc(x_in_loaded[h], 16)
                for h in range(2):
                    store_and_reload(b, h, True)
            for h in range(2):
                store_and_reload(B - 1, h, False)
            for h in range(2):
                sp.wait_ge(stored[h], 16 * (B + 1))

        @block.scalar
        def _(act):
            act.dma_start(ident[:], identity).then_inc(s["ident_in"], 16)
            act.dma_start(w1_sb[:], w1).then_inc(s["small_in"], 16)
            act.dma_start(gw_sb[:], gate_w).then_inc(s["gwt_in"], 16)
            act.dma_start(b1_col[:], b1.rearrange("(p o) -> p o", o=1)).then_inc(s["small_in"], 16)
            act.dma_start(w2_col[:], w2.rearrange("o p -> p o")).then_inc(s["small_in"], 16)
            act.dma_start(b2_sb[:], b2.rearrange("(p o) -> p o", o=1)).then_inc(s["small_in"], 16)
            act.dma_start(upto_sb[:], upto).then_inc(s["small_in"], 16)
            act.dma_start(gu_sb[:, 0:H], sw_gate).then_inc(s["shared_in"], 16)
            act.dma_start(gu_sb[:, H:2 * H], sw_up).then_inc(s["shared_in"], 16)
            act.dma_start(select_f[:], pair_select).then_inc(s["select_in"], 16)

            def shared_weights(b, h):
                act.wait_ge(s["shared_in"], 32)
                nc.scalar.copy(gu_hi[:, 0:2 * H], gu_sb[:, 0:2 * H]).then_inc(s["shared_hi"], 1)

            def gate_weights(b, h):
                act.wait_ge(s["gate_in"], 16)
                nc.scalar.copy(gu_hi[:, GATE], gu_sb[:, GATE]).then_inc(s["gu_hi_set"], 1)

            def up_weights(b, h):
                act.wait_ge(s["up_in"], 16)
                nc.scalar.copy(gu_hi[:, UP], gu_sb[:, UP]).then_inc(s["gu_hi_set"], 1)
                act.wait_ge(s["select_in"], 16)
                nc.scalar.copy(select[:], select_f[:]).then_inc(s["select_set"], 1)

            def down_weights(b, h):
                act.wait_ge(s["down_in"], 48)
                nc.scalar.copy(dn_hi[:], dn_sb[:]).then_inc(s["dn_hi_set"], 1)

            def norm1(b, h):
                n = half_no(b, h)
                act.wait_ge(s["scale1_set"], n + 1)
                for t in range(TILES):
                    last = nc.scalar.activation(xn[h][:, t, :], x_in[h][:, t, :], ACT.Identity,
                                                bias=shift1[h][:, t:t + 1], scale=rstd1[h][:, t:t + 1])
                last.then_inc(s["xn_set"], 1)

            def spread1(b, h):
                act.wait_ge(s["xnt_ps"], half_no(b, h) + 1)
                nc.scalar.copy(xnt_hi[:], BANK["spread1", h][:]).then_inc(s["xnt_hi_set"], 1)

            def hidden(b, h):
                act.wait_ge(s["hid_ps"], half_no(b, h) + 1)
                nc.scalar.activation(hid[:], BANK["hidden", h][:], ACT.Tanh, bias=b1_col[:, 0:1]).then_inc(s["hid_set"], 1)

            def weigh(b, h):
                n = half_no(b, h)
                act.wait_ge(s["weight_set"], b + 1)
                wait(act, "xwt_ps", n)
                for t in range(TILES):
                    last = nc.scalar.activation(xw[:, t, :], xn[h][:, t, :], ACT.Copy,
                                                scale=weight[:, h * TILES + t:h * TILES + t + 1])
                last.then_inc(s["xw_set"], 1)

            def norm2(b, h):
                n = half_no(b, h)
                act.wait_ge(s["scale2_set"], n + 1)
                wait(act, "xft_ps", n)
                for t in range(TILES):
                    last = nc.scalar.activation(xf[:, t, :], x_res[h][:, t, :], ACT.Identity,
                                                bias=shift2[h][:, t:t + 1], scale=rstd2[h][:, t:t + 1])
                last.then_inc(s["xf_set"], 1)

            def spread2(b, h):
                act.wait_ge(s["xft_ps"], half_no(b, h) + 1)
                nc.scalar.copy(xft_hi[h][:], BANK["spread2", h][:]).then_inc(s["xft_hi_set"], 1)

            def logits(b, h):
                act.wait_ge(s["logit_ps"], half_no(b, h) + 1)
                nc.scalar.copy(logit_t[:], BANK["logits", h][0:E, :]).then_inc(s["logit_set"], 1)

            def gates(b, h):
                n = half_no(b, h)
                act.wait_ge(s["logit_cols_ps"], n + 1)
                act.wait_ge(s["half_inv_set"], n + 1)
                wait(act, "comb_set", n)
                for t in range(TILES):
                    last = nc.scalar.activation(tanh_half[:, t, :], BANK["gates", h][:, t * E:(t + 1) * E],
                                                ACT.Tanh, scale=half_inv[h][:, t:t + 1])
                last.then_inc(s["tanh_set"], 1)

            def route(b, h):
                act.wait_ge(s["comb_ps"], half_no(b, h) + 1)
                nc.scalar.copy(comb_t[h][:], BANK["route", h][0:2 * E, :]).then_inc(s["comb_t_set"], 1)

            def hidden_high(b, h, i):
                if i == 0:
                    act.wait_ge(s["prod_set"], chunk_no(b, h, 1))
                    last = nc.scalar.copy(h_shared[0:H, :], hfull[(CHUNKS * h) % 2][0:H, :])
                else:
                    act.wait_ge(s["hfull_set"], PAIRS * half_no(b, h) + i)
                    last = nc.scalar.copy(h_hi[i % 3][:], hfull[(CHUNKS * h + i) % 2][:])
                last.then_inc(s["h_hi_set"], 1)

            def before(b, h, i):
                return (b, h, i - 1) if i else ((b, 0, CHUNKS - 1) if h else (b - 1, 1, CHUNKS - 1))

            def step(b, h, i):
                c = chunk_no(b, h, i)
                act.wait_ge(s["gate_ready"], c + 1)
                wait(act, "prod_set", c - 1)
                rows = slice(0, H if i == 0 else P)
                buf = (CHUNKS * h + i) % 2
                nc.scalar.activation(silu[buf][rows, :], ps_gate[buf][rows, :], ACT.Silu).then_inc(s["silu_set"], 1)
                if not (isinstance(c, int) and c == 0):
                    hidden_high(*before(b, h, i))

            def collect(b, h):
                act.wait_ge(s["down_done"], chunk_no(b, h, CHUNKS))
                nc.scalar.copy(y_t[:], ps_y[:]).then_inc(s["y_set"], 1)

            run(step, {"shared_weights": shared_weights, "gate_weights": gate_weights, "up_weights": up_weights,
                       "down_weights": down_weights, "norm1": norm1, "spread1": spread1, "hidden": hidden,
                       "weigh": weigh, "norm2": norm2, "spread2": spread2, "logits": logits, "gates": gates,
                       "route": route, "collect": collect}, act)
            hidden_high(B - 1, 1, CHUNKS - 1)
            collect(B - 1, 1)

        @block.gpsimd
        def _(pool):
            nc.gpsimd.memset(euler[:], 2.718281828459045).then_inc(s["consts_set"], 1)
            nc.gpsimd.memset(minus_half[:], -0.5).then_inc(s["consts_set"], 1)
            nc.gpsimd.memset(ones[:], 1.0).then_inc(s["consts_set"], 1)
            nc.gpsimd.memset(zeros[:], 0.0).then_inc(s["consts_set"], 1)
            nc.gpsimd.memset(tile_sums[:, 0:1], 0.0).then_inc(s["consts_set"], 1)
            nc.gpsimd.memset(gwt[:], 0.0).then_inc(s["gwt_zeroed"], 1)
            pool.wait_ge(s["consts_set"], 5)

            def small_weights(b, h):
                pool.wait_ge(s["gw_squared"], 2)
                nc.gpsimd.tensor_tensor(gw_inv[:], gw_n2[:], minus_half[0:E, 0:1], ALU.pow).then_inc(s["gw_scaled"], 1)

            def stats1(b, h):
                n = half_no(b, h)
                pool.wait_ge(s["stats1_set"], n + 1)
                nc.gpsimd.tensor_tensor(rstd1[h][:], var_eps1[h][:], minus_half[:], ALU.pow).then_inc(s["scale1_pool"], 1)
                pool.wait_ge(s["scale1_pool"], n + 1)
                nc.gpsimd.tensor_tensor(shift1[h][:], neg_mean1[h][:], rstd1[h][:], ALU.mult).then_inc(s["scale1_set"], 1)

            def softmax(b, h):
                pool.wait_ge(s["top_set"], b + 1)
                nc.gpsimd.tensor_tensor(own_score[:], score[:], zeros[:, 0:2 * TILES], ALU.add)
                nc.gpsimd.partition_all_reduce(top_all[:], top[:], P, bass.bass_isa.ReduceOp.max).then_inc(s["weight_pool"], 1)
                pool.wait_ge(s["weight_pool"], 2 * b + 1)
                nc.gpsimd.tensor_tensor(below[:], own_score[:], top_all[:].broadcast_to([P, 2 * TILES]),
                                        ALU.subtract).then_inc(s["weight_pool"], 1)
                pool.wait_ge(s["weight_pool"], 2 * b + 2)
                wait(pool, "xw_set", 2 * b)
                nc.gpsimd.tensor_tensor(weight[:], euler[:], below[:], ALU.pow).then_inc(s["weight_set"], 1)

            def attend(b, h):
                n = half_no(b, h)
                pool.wait_ge(s["stats2_set"], n + 1)
                nc.gpsimd.tensor_tensor(rstd2[h][:], var_eps2[h][:], minus_half[:], ALU.pow).then_inc(s["scale2_pool"], 1)
                pool.wait_ge(s["scale2_pool"], 4 * n + 1)
                nc.gpsimd.tensor_tensor(xf_norm[h][:], var512[h][:], rstd2[h][:], ALU.mult).then_inc(s["scale2_pool"], 1)
                pool.wait_ge(s["scale2_pool"], 4 * n + 2)
                nc.gpsimd.tensor_tensor(xf_norm2[h][:], xf_norm[h][:], rstd2[h][:], ALU.mult).then_inc(s["scale2_pool"], 1)
                pool.wait_ge(s["scale2_pool"], 4 * n + 3)
                nc.gpsimd.tensor_tensor(shift2[h][:], neg_mean2[h][:], rstd2[h][:], ALU.mult).then_inc(s["scale2_set"], 1)
                nc.gpsimd.tensor_scalar(xf_norm3[h][:], xf_norm2[h][:], 4 * NORM_EPS ** 2, None, ALU.max).then_inc(s["scale2_pool"], 1)
                pool.wait_ge(s["scale2_pool"], 4 * n + 4)
                nc.gpsimd.tensor_tensor(half_inv[h][:], xf_norm3[h][:], minus_half[:], ALU.pow).then_inc(s["half_inv_set"], 1)

            def hidden_low(b, h, i):
                if i == 0:
                    return
                pool.wait_ge(s["h_hi_set"], chunk_no(b, h, i) + 1)
                nc.gpsimd.tensor_tensor(h_lo[i % 3][:], hfull[(CHUNKS * h + i) % 2][:], word(h_hi[i % 3][:]),
                                        ALU.subtract).then_inc(s["h_lo_set"], 1)

            def step(b, h, i):
                if i:
                    hidden_low(b, h, i - 1)
                elif not (isinstance(b, int) and b == 0 and h == 0):
                    hidden_low(*((b, 0) if h else (b - 1, 1)), CHUNKS - 1)

            run(step, {"small_weights": small_weights, "stats1": stats1, "softmax": softmax, "attend": attend}, pool)
            hidden_low(B - 1, 1, CHUNKS - 1)

        @block.vector
        def _(dve):
            def low(out_, whole, hi, name):
                return nc.vector.tensor_tensor(out_, whole, word(hi), ALU.subtract).then_inc(s[name], 1)

            def small_weights(b, h):
                dve.wait_ge(s["gwt_in"], 16)
                nc.vector.scalar_tensor_tensor(out=gw_sq[:], in0=gw_sb[:], scalar=1.0, in1=gw_sb[:], op0=ALU.mult,
                                               op1=ALU.mult).then_inc(s["gw_squared"], 1)
                dve.wait_ge(s["gw_squared"], 1)
                nc.vector.tensor_reduce(gw_inv[:], gw_sq[:], AX.X, ALU.add).then_inc(s["gw_unit_set"], 1)
                dve.wait_ge(s["gw_unit_set"], 1)
                nc.vector.tensor_scalar(gw_n2[:], gw_inv[:], NORM_EPS ** 2, None, ALU.max).then_inc(s["gw_squared"], 1)
                dve.wait_ge(s["w1t_ps"], 1)
                nc.vector.tensor_copy(w1t[:], ps_a[:, 0:P]).then_inc(s["w1t_split"], 1)
                dve.wait_ge(s["w1t_split"], 1)
                nc.vector.tensor_copy(w1t_hi[:], w1t[:]).then_inc(s["w1t_split"], 1)
                dve.wait_ge(s["w1t_split"], 2)
                low(w1t_lo[:], w1t[:], w1t_hi[:], "w1t_split")
                dve.wait_ge(s["gw_scaled"], 1)
                nc.vector.tensor_scalar(gw_unit[:], gw_sb[:], gw_inv[:, 0:1], None, ALU.mult).then_inc(s["gw_unit_set"], 1)
                dve.wait_ge(s["gwt_zeroed"], 1)
                dve.wait_ge(s["gwt_ps"], 1)
                nc.vector.tensor_copy(gwt[:, 0:E], ps_b[:, 0:E]).then_inc(s["gwt_split"], 1)
                dve.wait_ge(s["gwt_split"], 1)
                nc.vector.tensor_copy(gwt_hi[:], gwt[:]).then_inc(s["gwt_split"], 1)
                dve.wait_ge(s["gwt_split"], 2)
                low(gwt_lo[:], gwt[:], gwt_hi[:], "gwt_split")

            def shared_weights(b, h):
                dve.wait_ge(s["shared_hi"], 1)
                low(gu_lo[:, 0:2 * H], gu_sb[:, 0:2 * H], gu_hi[:, 0:2 * H], "shared_lo")

            def gate_weights(b, h):
                dve.wait_ge(s["gu_hi_set"], 1)
                low(gu_lo[:, GATE], gu_sb[:, GATE], gu_hi[:, GATE], "gu_lo_set")

            def up_weights(b, h):
                dve.wait_ge(s["gu_hi_set"], 2)
                low(gu_lo[:, UP], gu_sb[:, UP], gu_hi[:, UP], "gu_lo_set")

            def down_weights(b, h):
                dve.wait_ge(s["dn_hi_set"], 1)
                low(dn_lo[:], dn_sb[:], dn_hi[:], "dn_lo_set")

            def moments(src, bn, mv, chain, n):
                for t in range(TILES):
                    last = nc.vector.bn_stats(bn[:, t, :], src[:, t, :])
                dve.drain()
                for t in range(TILES):
                    last = nc.vector.bn_aggr(mv[:, t, :], bn[:, t, :])
                last.then_inc(s[chain], 1)
                dve.wait_ge(s[chain], n + 1)

            def stats1(b, h):
                n = half_no(b, h)
                dve.wait_ge(x_in_loaded[h], 16 * b + 16)
                wait(dve, "xn_set", n - 1)
                moments(x_in[h], bn1[h], mv1[h], "stats1_dve", n)
                nc.vector.tensor_scalar(neg_mean1[h][:], mv1[h][:, :, 0], -1.0, None, ALU.mult)
                nc.vector.tensor_scalar(var_eps1[h][:], mv1[h][:, :, 1], EPS, None, ALU.add).then_inc(s["stats1_set"], 1)

            def spread1(b, h):
                dve.wait_ge(s["xnt_hi_set"], half_no(b, h) + 1)
                low(xnt_lo[:], BANK["spread1", h][:], xnt_hi[:], "xnt_lo_set")

            def score_stage(b, h):
                n = half_no(b, h)
                dve.wait_ge(s["score_ps"], n + 1)
                if h == 0:
                    wait(dve, "score_cols_ps", b)
                nc.vector.tensor_scalar(score_row[h][:], BANK["score", h][0:1, :], b2_sb[0:1, 0:1], None,
                                        ALU.add).then_inc(s["score_row_set"], 1)

            def softmax(b, h):
                dve.wait_ge(s["score_cols_ps"], b + 1)
                wait(dve, "weight_set", b)
                nc.vector.tensor_copy(score[:], BANK["softmax", 0][:, 0:2 * TILES]).then_inc(s["score_dve"], 1)
                dve.wait_ge(s["score_dve"], b + 1)
                nc.vector.tensor_reduce(top[:], score[:], AX.X, ALU.max).then_inc(s["top_set"], 1)

            def sums(b, h):
                dve.wait_ge(s["weight_set"], b + 1)
                nc.vector.tensor_tensor_scan(tile_sums[:, 1:2 * TILES + 1], weight[:], zeros[:, 0:2 * TILES],
                                             0.0, ALU.add, ALU.add).then_inc(s["sums_set"], 1)

            def denominator(b, h):
                dve.wait_ge(s["den_ps"], b + 1)
                nc.vector.reciprocal(inv_den[:], BANK["denominator", 0][:, 0:2 * TILES]).then_inc(s["inv_den_set"], 1)

            def scan(b, h):
                n = half_no(b, h)
                dve.wait_ge(s["xwt_ps"], n + 1)
                if h == 1:
                    dve.wait_ge(s["num_set"], n)
                wait(dve, "num_ps", n - 1)
                start = num_t[0][:, HALF - 1:HALF] if h else 0.0
                nc.vector.tensor_tensor_scan(num_t[h][:], zeros[:], BANK["scan", h][:], start, ALU.add,
                                             ALU.add).then_inc(s["num_set"], 1)

            def attend(b, h):
                n = half_no(b, h)
                dve.wait_ge(s["num_ps"], n + 1)
                dve.wait_ge(s["inv_den_set"], b + 1)
                dve.wait_ge(x_res_loaded[h], 16 * b + 16)
                for t in range(TILES):
                    col = h * TILES + t
                    last = nc.vector.scalar_tensor_tensor(
                        out=x_res[h][:, t, :], in0=BANK["attend", h][:, tile(t)], scalar=inv_den[:, col:col + 1],
                        in1=x_res[h][:, t, :], op0=ALU.mult, op1=ALU.add)
                last.then_inc(s["attended"], 1)
                dve.wait_ge(s["attended"], n + 1)
                moments(x_res[h], bn2[h], mv2[h], "stats2_dve", n)
                nc.vector.tensor_scalar(neg_mean2[h][:], mv2[h][:, :, 0], -1.0, None, ALU.mult)
                nc.vector.tensor_scalar(var512[h][:], mv2[h][:, :, 1], 4.0 * D, None, ALU.mult)
                nc.vector.tensor_scalar(var_eps2[h][:], mv2[h][:, :, 1], EPS, None, ALU.add).then_inc(s["stats2_set"], 1)

            def spread2(b, h):
                dve.wait_ge(s["xft_hi_set"], half_no(b, h) + 1)
                low(xft_lo[h][:], BANK["spread2", h][:], xft_hi[h][:], "xft_lo_set")

            def gates(b, h):
                n = half_no(b, h)
                chain = [0]

                def link(ins):
                    ins.then_inc(s["route_dve"], 1)
                    chain[0] += 1
                    dve.wait_ge(s["route_dve"], 5 * n + chain[0])

                dve.wait_ge(s["tanh_set"], n + 1)
                nc.vector.tensor_scalar(gate[:], tanh_half[:], 0.5, 0.5, ALU.mult, ALU.add)
                dve.drain()
                for t in range(TILES):
                    nc.vector.max(best[:, t, :], gate[:, t, :])
                dve.drain()
                for t in range(TILES):
                    last = nc.vector.match_replace(struck[:, t, :], best[:, t, :], gate[:, t, :], -1.0)
                link(last)
                nc.vector.scalar_tensor_tensor(out=chosen[:], in0=struck[:], scalar=0.0, in1=gate[:],
                                               op0=ALU.is_lt, op1=ALU.mult)
                link(nc.vector.tensor_reduce(best_sum[:], best[:], AX.X, ALU.add))
                link(nc.vector.reciprocal(inv_best[:], best_sum[:]))
                link(nc.vector.tensor_tensor(comb[:], chosen[:], inv_best[:].unsqueeze(2).broadcast_to([P, TILES, E]),
                                             ALU.mult))
                wait(dve, "comb_ps", n)
                link(nc.vector.tensor_copy(comb_hl[:, :, 0:E], comb[:]))
                nc.vector.tensor_tensor(comb_hl[:, :, E:2 * E], comb[:], word(comb_hl[:, :, 0:E]),
                                        ALU.subtract).then_inc(s["comb_set"], 1)

            def step(b, h, i):
                c = chunk_no(b, h, i)
                n = half_no(b, h)
                buf = (CHUNKS * h + i) % 2
                dve.wait_ge(s["silu_set"], c + 1)
                if i == 0:
                    wait(dve, "h_lo_set", PAIRS * n - 1)
                    nc.vector.tensor_tensor(hfull[buf][0:H, :], silu[buf][0:H, :], ps_gate[buf][H:P, :],
                                            ALU.mult).then_inc(s["prod_set"], 1)
                    return
                dve.wait_ge(s["up_ready"], PAIRS * n + i)
                nc.vector.tensor_tensor(prod[buf][:], silu[buf][:], ps_up[buf][:], ALU.mult).then_inc(s["prod_set"], 1)
                dve.wait_ge(s["comb_ready"], PAIRS * n + i)
                dve.wait_ge(s["prod_set"], c + 1)
                if i == 2:
                    dve.wait_ge(s["shared_lo_set"], n + 1)
                elif i == 1:
                    wait(dve, "h_lo_set", PAIRS * n)
                else:
                    dve.wait_ge(s["h_lo_set"], PAIRS * n + i - 2)
                nc.vector.tensor_tensor(hfull[buf][:], prod[buf][:], ps_comb[:], ALU.mult).then_inc(s["hfull_set"], 1)
                if i == 1:
                    dve.wait_ge(s["h_hi_set"], chunk_no(b, h, 1))
                    low(h_shared[H:P, :], hfull[1 - buf][0:H, :], h_shared[0:H, :], "shared_lo_set")

            def out_stage(b, h):
                dve.wait_ge(s["out_ps"], half_no(b, h) + 1)
                dve.wait_ge(stored[h], 16 * b + 16)
                nc.vector.tensor_tensor(result[h][:].rearrange("p t d -> p (t d)"), BANK["out", h][:],
                                        x_res[h][:].rearrange("p t d -> p (t d)"), ALU.add).then_inc(s["result_set"], 1)

            for h in range(2):
                nc.vector.memset(result[h][:, 0, 0:1], 0.0).then_inc(stored[h], 16)
            run(step, {"small_weights": small_weights, "shared_weights": shared_weights,
                       "gate_weights": gate_weights, "up_weights": up_weights, "down_weights": down_weights,
                       "stats1": stats1, "spread1": spread1, "score": score_stage, "softmax": softmax, "sums": sums,
                       "denominator": denominator, "scan": scan, "attend": attend, "spread2": spread2,
                       "gates": gates, "out": out_stage}, dve)
            out_stage(B - 1, 1)

        @block.tensor
        def _(pe):
            mm = nc.tensor.matmul

            def split_product(out_, w_hi, w_lo, m_hi, m_lo, start=True, stop=True):
                mm(out_, w_hi, m_lo, start=start, stop=False)
                mm(out_, w_lo, m_hi, start=False, stop=False)
                return mm(out_, w_hi, m_hi, start=False, stop=stop)

            def transposes(out_, src):
                for t in range(TILES):
                    last = nc.tensor.transpose(out_[:, tile(t)], src(t), ident[:])
                return last

            def turn(t, out_, src, eye):
                if t == 0:
                    return mm(out_, src, eye, start=True, stop=True)
                return nc.tensor.transpose(out_, src, eye)

            def is_int(b, value):
                return isinstance(b, int) and b == value

            def small_weights(b, h):
                pe.wait_ge(s["ident_in"], 16)
                pe.wait_ge(s["small_in"], 16 * 5)
                nc.tensor.transpose(ps_a[:, 0:P], w1_sb[:], ident[:]).then_inc(s["w1t_ps"], 1)
                pe.wait_ge(s["gw_unit_set"], 2)
                nc.tensor.transpose(ps_b[:, 0:E], gw_unit[:], ident[0:E, 0:E]).then_inc(s["gwt_ps"], 1)

            def spread1(b, h):
                pe.wait_ge(s["xn_set"], half_no(b, h) + 1)
                if is_int(b, 0):
                    pe.wait_ge(s["w1t_split" if h else "gwt_split"], 1)
                elif h:
                    pe.wait_ge(s["logit_set"], 2 * b)
                transposes(BANK["spread1", h], lambda t: xn[h][:, t, :]).then_inc(s["xnt_ps"], 1)

            def hidden(b, h):
                pe.wait_ge(s["xnt_lo_set"], half_no(b, h) + 1)
                if is_int(b, 0) and h == 0:
                    pe.wait_ge(s["w1t_split"], 3)
                split_product(BANK["hidden", h][:], w1t_hi[:], w1t_lo[:], xnt_hi[:],
                              xnt_lo[:]).then_inc(s["hid_ps"], 1)

            def score_stage(b, h):
                pe.wait_ge(s["hid_set"], half_no(b, h) + 1)
                mm(BANK["score", h][0:1, :], w2_col[:], hid[:], start=True, stop=True).then_inc(s["score_ps"], 1)

            def softmax(b, h):
                pe.wait_ge(s["score_row_set"], 2 * b + 2)
                for t in range(2 * TILES):
                    last = turn(t, BANK["softmax", 0][:, t:t + 1], score_row[t // TILES][:, tile(t % TILES)],
                                ident[0:1, 0:1])
                last.then_inc(s["score_cols_ps"], 1)

            def scan(b, h):
                pe.wait_ge(s["xw_set"], half_no(b, h) + 1)
                transposes(BANK["scan", h], lambda t: xw[:, t, :]).then_inc(s["xwt_ps"], 1)

            def denominator(b, h):
                pe.wait_ge(s["sums_set"], b + 1)
                if not is_int(b, 0):
                    pe.wait_ge(s["result_set"], 2 * b - 1)
                den = BANK["denominator", 0][:, 0:2 * TILES]
                mm(den, ones[:], tile_sums[:, 0:2 * TILES], start=True, stop=False)
                mm(den, upto_sb[:], weight[:], start=False, stop=True).then_inc(s["den_ps"], 1)

            def attend(b, h):
                pe.wait_ge(s["num_set"], half_no(b, h) + 1)
                transposes(BANK["attend", h], lambda t: num_t[h][:, tile(t)]).then_inc(s["num_ps"], 1)

            def spread2(b, h):
                pe.wait_ge(s["xf_set"], half_no(b, h) + 1)
                transposes(BANK["spread2", h], lambda t: xf[:, t, :]).then_inc(s["xft_ps"], 1)

            def logits(b, h):
                pe.wait_ge(s["xft_lo_set"], half_no(b, h) + 1)
                if is_int(b, 0) and h == 0:
                    pe.wait_ge(s["gwt_split"], 3)
                split_product(BANK["logits", h][:], gwt_hi[:], gwt_lo[:], xft_hi[h][:],
                              xft_lo[h][:]).then_inc(s["logit_ps"], 1)

            def gates(b, h):
                pe.wait_ge(s["logit_set"], half_no(b, h) + 1)
                if h and not is_int(b, B - 1):
                    pe.wait_ge(s["score_row_set"], 2 * b + 3)
                for t in range(TILES):
                    last = turn(t, BANK["gates", h][:, t * E:(t + 1) * E], logit_t[:, tile(t)], ident[0:E, 0:E])
                last.then_inc(s["logit_cols_ps"], 1)

            def route(b, h):
                pe.wait_ge(s["comb_set"], half_no(b, h) + 1)
                for t in range(TILES):
                    last = nc.tensor.transpose(BANK["route", h][0:2 * E, tile(t)], word(comb_hl[:, t, :]), ident[:])
                last.then_inc(s["comb_ps"], 1)

            def out_stage(b, h):
                pe.wait_ge(s["y_set"], half_no(b, h) + 1)
                transposes(BANK["out", h], lambda t: y_t[:, tile(t)]).then_inc(s["out_ps"], 1)

            def down(b, h, i):
                n = half_no(b, h)
                cols = slice(i * D, (i + 1) * D)
                pe.wait_ge(s["h_hi_set"], chunk_no(b, h, i) + 1)
                if i == 0:
                    pe.wait_ge(s["shared_lo_set"], n + 1)
                    wait(pe, "y_set", n)
                    if is_int(b, 0) and h == 0:
                        pe.wait_ge(s["dn_lo_set"], 1)
                    mm(ps_y[:], dn_lo[:, cols], h_shared[:], start=True, stop=False)
                    last = mm(ps_y[:], dn_hi[:, cols], h_shared[:], start=False, stop=False)
                else:
                    pe.wait_ge(s["h_lo_set"], PAIRS * n + i)
                    last = split_product(ps_y[:], dn_hi[:, cols], dn_lo[:, cols], h_hi[i % 3][:], h_lo[i % 3][:],
                                         start=False, stop=i == CHUNKS - 1)
                last.then_inc(s["down_done"], 1)

            def step(b, h, i):
                c = chunk_no(b, h, i)
                n = half_no(b, h)
                buf = (CHUNKS * h + i) % 2
                if i == 0:
                    pe.wait_ge(s["xft_lo_set"], n + 1)
                    if is_int(b, 0) and h == 0:
                        pe.wait_ge(s["shared_lo"], 1)
                if i == 1 and is_int(b, 0) and h == 0:
                    pe.wait_ge(s["gu_lo_set"], 2)
                    pe.wait_ge(s["select_set"], 1)
                wait(pe, "prod_set", c - 1)

                def from_x(bank, first):
                    cols = slice(first, first + P)
                    return split_product(bank[:], gu_hi[:, cols], gu_lo[:, cols], xft_hi[h][:], xft_lo[h][:])

                if i == 0:
                    from_x(ps_gate[buf], 0).then_inc(s["gate_ready"], 1)
                else:
                    from_x(ps_gate[buf], GATE.start + (i - 1) * P).then_inc(s["gate_ready"], 1)
                    from_x(ps_up[buf], UP.start + (i - 1) * P).then_inc(s["up_ready"], 1)
                    if i == 1:
                        pe.wait_ge(s["comb_t_set"], n + 1)
                    wait(pe, "hfull_set", PAIRS * n + i - 1)
                    mm(ps_comb[:], select[:, (i - 1) * P:i * P], comb_t[h][:], start=True,
                       stop=True).then_inc(s["comb_ready"], 1)
                if i >= LAG:
                    down(b, h, i - LAG)
                elif h:
                    down(b, 0, CHUNKS + i - LAG)
                elif not is_int(b, 0):
                    down(b - 1, 1, CHUNKS + i - LAG)

            run(step, {"small_weights": small_weights, "spread1": spread1, "hidden": hidden, "score": score_stage,
                       "softmax": softmax, "scan": scan, "denominator": denominator, "attend": attend,
                       "spread2": spread2, "logits": logits, "gates": gates, "route": route, "out": out_stage},
                pe, stages_first=True)
            for i in range(CHUNKS - LAG, CHUNKS):
                down(B - 1, 1, i)
            out_stage(B - 1, 1)


_INS = ["L0_attn_x", "L0_attn_W1", "L0_attn_b1_", "L0_attn_W2", "L0_attn_b2_", "L0_ffn_gate_w", "L0_ffn_w_gate",
        "L0_ffn_w_up", "L0_ffn_w_down", "L0_ffn_sw_gate", "L0_ffn_sw_up", "L0_ffn_sw_down"]


def kernel(**inputs):
    import numpy as np
    import concourse.bacc as bacc
    from concourse.bass_utils import run_bass_kernel_spmd

    arrays = {f"in_{name}": np.ascontiguousarray(inputs[name]) for name in _INS}
    arrays["identity"] = np.eye(P, dtype=np.float32)
    arrays["pair_select"] = np.tile(np.kron(np.eye(E, dtype=np.float32), np.ones((1, H), np.float32)), (2, 1))
    arrays["upto"] = np.triu(np.ones((P, P), np.float32))
    nc = bacc.Bacc("TRN2", target_bir_lowering=False, num_devices=1)
    args = [nc.dram_tensor(name, a.shape, mybir.dt.from_np(a.dtype), kind="ExternalInput").ap()
            for name, a in arrays.items()]
    result = nc.dram_tensor("out_dram", (B, T, D), mybir.dt.float32, kind="ExternalOutput").ap()
    attention_moe_kernel(nc, *args, result)
    r = run_bass_kernel_spmd(nc, [arrays], core_ids=[0])
    return r.results[0]["out_dram"]
```

```python
import concourse.bass as bass
from concourse import mybir
from contextlib import ExitStack

B, T, D = 4, 1024, 128
E, H, K = 16, 64, 8
P = 128
HALF = T // 2
TILES = HALF // P
PAIRS = E // 2
CHUNKS = 1 + PAIRS
STEPS = 2 * CHUNKS
LAG = 2
EPS = 1e-5
NORM_EPS = 1e-12
GU = 2 * H + 2 * E * H
GATE = slice(2 * H, 2 * H + E * H)
UP = slice(2 * H + E * H, GU)

STAGES = {
    "pe": {
        0: [("route", 0, 0), ("score", 1, 0)],
        2: [("out", -1, 1), ("scan", 0, 1)],
        3: [("attend", 0, 1), ("spread1", 1, 1)],
        4: [("hidden", 1, 1)],
        5: [("score", 1, 1), ("spread2", 0, 1)],
        6: [("softmax", 1, 0), ("logits", 0, 1)],
        7: [("gates", 0, 1)],
        8: [("denominator", 1, 0)],
        9: [("route", 0, 1)],
        10: [("scan", 1, 0)],
        11: [("out", 0, 0)],
        12: [("attend", 1, 0)],
        14: [("spread2", 1, 0)],
        15: [("logits", 1, 0)],
        16: [("gates", 1, 0), ("spread1", 2, 0)],
        17: [("hidden", 2, 0)],
    },
    "act": {
        0: [("route", 0, 0), ("weigh", 0, 1)],
        1: [("collect", -1, 1), ("score", 1, 0)],
        2: [("norm1", 1, 1)],
        3: [("spread1", 1, 1)],
        4: [("hidden", 1, 1), ("norm2", 0, 1)],
        5: [("spread2", 0, 1), ("score", 1, 1)],
        6: [("logits", 0, 1)],
        7: [("gates", 0, 1)],
        9: [("route", 0, 1), ("weigh", 1, 0)],
        10: [("collect", 0, 0)],
        13: [("norm2", 1, 0)],
        14: [("spread2", 1, 0)],
        15: [("logits", 1, 0), ("norm1", 2, 0)],
        16: [("gates", 1, 0), ("spread1", 2, 0)],
        17: [("hidden", 2, 0)],
    },
    "pool": {
        0: [("stats1", 1, 1)],
        3: [("attend", 0, 1)],
        6: [("softmax", 1, 0)],
        12: [("attend", 1, 0)],
        13: [("stats1", 2, 0)],
    },
    "dve": {
        0: [("stats1", 1, 1)],
        2: [("out", -1, 1), ("scan", 0, 1)],
        3: [("attend", 0, 1), ("spread1", 1, 1)],
        5: [("spread2", 0, 1)],
        6: [("softmax", 1, 0)],
        7: [("sums", 1, 0)],
        8: [("gates", 0, 1), ("denominator", 1, 0)],
        10: [("scan", 1, 0)],
        11: [("out", 0, 0)],
        12: [("attend", 1, 0)],
        13: [("stats1", 2, 0)],
        14: [("spread2", 1, 0)],
        16: [("spread1", 2, 0)],
        17: [("gates", 1, 0)],
    },
}
FIRST_STAGES = [
    ("small_weights", 0, 0), ("stats1", 0, 0), ("norm1", 0, 0), ("stats1", 0, 1), ("norm1", 0, 1),
    ("spread1", 0, 0), ("hidden", 0, 0), ("score", 0, 0), ("spread1", 0, 1), ("shared_weights", 0, 0),
    ("hidden", 0, 1), ("score", 0, 1), ("softmax", 0, 0), ("gate_weights", 0, 0), ("sums", 0, 0), ("weigh", 0, 0),
    ("denominator", 0, 0), ("scan", 0, 0), ("attend", 0, 0), ("norm2", 0, 0), ("up_weights", 0, 0),
    ("spread2", 0, 0), ("logits", 0, 0), ("stats1", 1, 0), ("norm1", 1, 0), ("gates", 0, 0),
    ("down_weights", 0, 0), ("spread1", 1, 0), ("hidden", 1, 0),
]
HEAD = 3
AHEAD = 2


def attention_moe_kernel(nc: bass.Bass, x, w1, b1, w2, b2, gate_w, w_gate, w_up, w_down,
                         sw_gate, sw_up, sw_down, identity, pair_select, upto, out):
    f32 = mybir.dt.float32
    f32r = mybir.dt.float32r
    ALU = mybir.AluOpType
    ACT = mybir.ActivationFunctionType
    AX = mybir.AxisListType

    ctx = ExitStack()
    with ctx:
        def sb(name, shape, dt=f32):
            return ctx.enter_context(nc.sbuf_tensor(name, shape, dt))

        def pb(name):
            return ctx.enter_context(nc.psum_tensor(name, [P, HALF], f32))

        def sem(name):
            return ctx.enter_context(nc.semaphore(name))

        def word(ap):
            return ap.bitcast(f32)

        ident = sb("ident", [P, P])
        upto_sb = sb("upto_sb", [P, P])
        ones = sb("ones", [P, P])
        select_f = sb("select_f", [2 * E, PAIRS * P])
        select = sb("select", [2 * E, PAIRS * P], f32r)
        w1_sb = sb("w1_sb", [P, D])
        w1t = sb("w1t", [P, P])
        w1t_hi, w1t_lo = sb("w1t_hi", [P, P], f32r), sb("w1t_lo", [P, P], f32r)
        w2_col = sb("w2_col", [P, 1])
        b1_col = sb("b1_col", [P, 1])
        b2_sb = sb("b2_sb", [1, 1])
        gw_sb = sb("gw_sb", [E, D])
        gw_sq = sb("gw_sq", [E, D])
        gw_n2 = sb("gw_n2", [E, 1])
        gw_inv = sb("gw_inv", [E, 1])
        gw_unit = sb("gw_unit", [E, D])
        gwt = sb("gwt", [P, P])
        gwt_hi, gwt_lo = sb("gwt_hi", [P, P], f32r), sb("gwt_lo", [P, P], f32r)
        gu_sb = sb("gu_sb", [P, GU])
        gu_hi, gu_lo = sb("gu_hi", [P, GU], f32r), sb("gu_lo", [P, GU], f32r)
        dn_sb = sb("dn_sb", [P, CHUNKS * D])
        dn_hi, dn_lo = sb("dn_hi", [P, CHUNKS * D], f32r), sb("dn_lo", [P, CHUNKS * D], f32r)
        euler = sb("euler", [P, 2 * TILES])
        minus_half = sb("minus_half", [P, TILES])
        zeros = sb("zeros", [P, HALF])

        def pair(name, shape, dt=f32):
            return [sb(f"{name}{h}", shape, dt) for h in range(2)]

        x_in = pair("x_in", [P, TILES, D])
        x_raw = pair("x_raw", [P, TILES, D])
        x_att = pair("x_att", [P, TILES, D])
        xn = pair("xn", [P, TILES, D])
        bn1, bn2 = pair("bn1_", [P, TILES, 6]), pair("bn2_", [P, TILES, 6])
        mv1, mv2 = pair("mv1_", [P, TILES, 2]), pair("mv2_", [P, TILES, 2])
        var_eps1, var_eps2 = pair("var_eps1_", [P, TILES]), pair("var_eps2_", [P, TILES])
        neg_mean1, neg_mean2 = pair("neg_mean1_", [P, TILES]), pair("neg_mean2_", [P, TILES])
        rstd1, rstd2 = pair("rstd1_", [P, TILES]), pair("rstd2_", [P, TILES])
        shift1, shift2 = pair("shift1_", [P, TILES]), pair("shift2_", [P, TILES])
        var512 = pair("var512_", [P, TILES])
        xf_norm = pair("xf_norm", [P, TILES])
        xf_norm2 = pair("xf_norm2_", [P, TILES])
        xf_norm3 = pair("xf_norm3_", [P, TILES])
        half_inv = pair("half_inv", [P, TILES])
        xnt_hi, xnt_lo = sb("xnt_hi", [P, HALF], f32r), sb("xnt_lo", [P, HALF], f32r)
        hid = sb("hid", [P, HALF])
        score_row = pair("score_row", [1, HALF])
        score = sb("score", [P, 2 * TILES])
        top = sb("top", [P, 1])
        own_score = sb("own_score", [P, 2 * TILES])
        top_all = sb("top_all", [P, 1])
        below = sb("below", [P, 2 * TILES])
        weight = sb("weight", [P, 2 * TILES])
        tile_sums = sb("tile_sums", [P, 2 * TILES + 1])
        inv_den = sb("inv_den", [P, 2 * TILES])
        xw = sb("xw", [P, TILES, D])
        num_t = pair("num_t", [P, HALF])
        xf = sb("xf", [P, TILES, D])
        xft_hi, xft_lo = pair("xft_hi", [P, HALF], f32r), pair("xft_lo", [P, HALF], f32r)

        logit_t = sb("logit_t", [E, HALF])
        tanh_half = sb("tanh_half", [P, TILES, E])
        gate = sb("gate", [P, TILES, E])
        best = sb("best", [P, TILES, K])
        struck = sb("struck", [P, TILES, E])
        chosen = sb("chosen", [P, TILES, E])
        best_sum = sb("best_sum", [P, TILES])
        inv_best = sb("inv_best", [P, TILES])
        comb = sb("comb", [P, TILES, E])
        comb_hl = sb("comb_hl", [P, TILES, 2 * E], f32r)
        comb_t = pair("comb_t", [2 * E, HALF], f32r)

        silu = [sb(f"silu{i}", [P, HALF]) for i in range(2)]
        prod = [sb(f"prod{i}", [P, HALF]) for i in range(2)]
        hfull = [sb(f"hfull{i}", [P, HALF]) for i in range(2)]
        h_hi = [sb(f"h_hi{i}", [P, HALF], f32r) for i in range(3)]
        h_lo = [sb(f"h_lo{i}", [P, HALF], f32r) for i in range(3)]
        h_shared = sb("h_shared", [P, HALF], f32r)
        y_t = sb("y_t", [P, HALF])
        result = pair("result", [P, TILES, D])

        ps_gate = [pb("ps_gate0"), pb("ps_gate1")]
        ps_up = [pb("ps_up0"), pb("ps_up1")]
        ps_comb = pb("ps_comb")
        ps_y = pb("ps_y")
        ps_a = pb("ps_a")
        ps_b = pb("ps_b")

        BANK = {}
        for stage, first, second in (
                ("spread1", ps_b, ps_a), ("hidden", ps_b, ps_a), ("score", ps_b, ps_a), ("softmax", ps_a, None),
                ("denominator", ps_a, None), ("scan", ps_a, ps_a), ("attend", ps_a, ps_b), ("spread2", ps_b, ps_b),
                ("logits", ps_a, ps_b), ("gates", ps_a, ps_b), ("route", ps_a, ps_b), ("out", ps_b, ps_b)):
            BANK[stage, 0], BANK[stage, 1] = first, second

        names = """ident_in small_in gwt_in select_in shared_in gate_in up_in down_in
            consts_set w1t_ps w1t_split gw_squared gw_scaled gw_unit_set gwt_ps gwt_split gwt_zeroed
            select_set shared_hi shared_lo gu_hi_set gu_lo_set dn_hi_set dn_lo_set
            stats1_dve stats1_set scale1_pool scale1_set xn_set xnt_ps xnt_hi_set xnt_lo_set
            hid_ps hid_set score_ps score_row_set score_cols_ps score_dve top_set weight_pool
            weight_set sums_set den_ps inv_den_set xw_set xwt_ps num_set num_ps attended
            stats2_dve stats2_set scale2_pool scale2_set half_inv_set xf_set xft_ps xft_hi_set
            xft_lo_set logit_ps logit_set logit_cols_ps tanh_set route_dve comb_set comb_ps
            comb_t_set gate_ready up_ready comb_ready silu_set prod_set hfull_set h_hi_set
            h_lo_set shared_lo_set down_done y_set out_ps result_set""".split()
        s = {n: sem(n) for n in names}
        x_in_loaded = [sem("x_in_loaded0"), sem("x_in_loaded1")]
        x_raw_loaded = [sem("x_raw_loaded0"), sem("x_raw_loaded1")]
        stored = [sem("stored0"), sem("stored1")]

        block = ctx.enter_context(nc.Block())

        def half_no(b, h):
            return 2 * b + h

        def chunk_no(b, h, i):
            return STEPS * b + CHUNKS * h + i

        def wait(eng, name, value):
            if not isinstance(value, int) or value > 0:
                eng.wait_ge(s[name], value)

        def run(engine, step, stages, eng):
            for name, b, h in FIRST_STAGES:
                if name in stages:
                    stages[name](b, h)

            def steps(b, first, last, ahead):
                for n in range(first, last):
                    def between():
                        for name, off, h in STAGES[engine].get(n, ()):
                            if off <= ahead and not (off < 0 and isinstance(b, int) and b == 0):
                                stages[name](b + off, h)
                    step(b, n // CHUNKS, n % CHUNKS, between)

            steps(0, 0, HEAD, AHEAD)
            with eng.Fori(0, B - AHEAD) as b:
                steps(b, HEAD, STEPS, AHEAD)
                steps(b + 1, 0, HEAD, AHEAD)
            for b in range(B - AHEAD, B):
                steps(b, HEAD, STEPS, B - 1 - b)
                if b + 1 < B:
                    steps(b + 1, 0, HEAD, B - 2 - b)

        def tile(t):
            return slice(t * P, (t + 1) * P)

        @block.sync
        def _(sp):
            def rows(src, b, h):
                return src[b, h * HALF:(h + 1) * HALF, :].rearrange("(t p) d -> p t d", p=P)

            sp.dma_start(x_in[0][:], rows(x, 0, 0)).then_inc(x_in_loaded[0], 16)
            sp.dma_start(x_in[1][:], rows(x, 0, 1)).then_inc(x_in_loaded[1], 16)
            sp.dma_start(gu_sb[:, 2 * H:2 * H + E * H].rearrange("d (e h) -> d e h", e=E),
                         w_gate.rearrange("e d h -> d e h")).then_inc(s["gate_in"], 16)
            sp.dma_start(gu_sb[:, 2 * H + E * H:GU].rearrange("d (e h) -> d e h", e=E),
                         w_up.rearrange("e d h -> d e h")).then_inc(s["up_in"], 16)
            sp.dma_start(x_raw[0][:], rows(x, 0, 0)).then_inc(x_raw_loaded[0], 16)
            sp.dma_start(x_raw[1][:], rows(x, 0, 1)).then_inc(x_raw_loaded[1], 16)
            sp.dma_start(dn_sb[:, D:].rearrange("p (c d) -> p c d", c=PAIRS),
                         w_down.rearrange("(c e) h d -> (e h) c d", c=PAIRS)).then_inc(s["down_in"], 16)
            sp.dma_start(dn_sb[0:H, 0:D], sw_down).then_inc(s["down_in"], 16)
            sp.dma_start(dn_sb[H:P, 0:D], sw_down).then_inc(s["down_in"], 16)

            def load_in(b):
                for h in range(2):
                    sp.wait_ge(s["xn_set"], half_no(b - 1, h) + 1)
                    sp.dma_start(x_in[h][:], rows(x, b, h)).then_inc(x_in_loaded[h], 16)

            def load_raw(b):
                for h in range(2):
                    sp.wait_ge(s["attended"], half_no(b - 1, h) + 1)
                    sp.dma_start(x_raw[h][:], rows(x, b, h)).then_inc(x_raw_loaded[h], 16)

            def store(b):
                for h in range(2):
                    sp.wait_ge(s["result_set"], half_no(b, h) + 1)
                    sp.dma_start(rows(out, b, h), result[h][:]).then_inc(stored[h], 16)

            load_in(1)
            with sp.Fori(0, B - AHEAD) as b:
                load_raw(b + 1)
                load_in(b + 2)
                store(b)
            load_raw(B - 1)
            store(B - 2)
            store(B - 1)
            for h in range(2):
                sp.wait_ge(stored[h], 16 * (B + 1))

        @block.scalar
        def _(act):
            act.dma_start(ident[:], identity).then_inc(s["ident_in"], 16)
            act.dma_start(w1_sb[:], w1).then_inc(s["small_in"], 16)
            act.dma_start(gw_sb[:], gate_w).then_inc(s["gwt_in"], 16)
            act.dma_start(b1_col[:], b1.rearrange("(p o) -> p o", o=1)).then_inc(s["small_in"], 16)
            act.dma_start(w2_col[:], w2.rearrange("o p -> p o")).then_inc(s["small_in"], 16)
            act.dma_start(b2_sb[:], b2.rearrange("(p o) -> p o", o=1)).then_inc(s["small_in"], 16)
            act.dma_start(upto_sb[:], upto).then_inc(s["small_in"], 16)
            act.dma_start(gu_sb[:, 0:H], sw_gate).then_inc(s["shared_in"], 16)
            act.dma_start(gu_sb[:, H:2 * H], sw_up).then_inc(s["shared_in"], 16)
            act.dma_start(select_f[:], pair_select).then_inc(s["select_in"], 16)

            def shared_weights(b, h):
                act.wait_ge(s["shared_in"], 32)
                nc.scalar.copy(gu_hi[:, 0:2 * H], gu_sb[:, 0:2 * H]).then_inc(s["shared_hi"], 1)

            def gate_weights(b, h):
                act.wait_ge(s["gate_in"], 16)
                nc.scalar.copy(gu_hi[:, GATE], gu_sb[:, GATE]).then_inc(s["gu_hi_set"], 1)

            def up_weights(b, h):
                act.wait_ge(s["up_in"], 16)
                nc.scalar.copy(gu_hi[:, UP], gu_sb[:, UP]).then_inc(s["gu_hi_set"], 1)
                act.wait_ge(s["select_in"], 16)
                nc.scalar.copy(select[:], select_f[:]).then_inc(s["select_set"], 1)

            def down_weights(b, h):
                act.wait_ge(s["down_in"], 48)
                nc.scalar.copy(dn_hi[:], dn_sb[:]).then_inc(s["dn_hi_set"], 1)

            def norm1(b, h):
                n = half_no(b, h)
                act.wait_ge(s["scale1_set"], n + 1)
                for t in range(TILES):
                    last = nc.scalar.activation(xn[h][:, t, :], x_in[h][:, t, :], ACT.Identity,
                                                bias=shift1[h][:, t:t + 1], scale=rstd1[h][:, t:t + 1])
                last.then_inc(s["xn_set"], 1)

            def spread1(b, h):
                act.wait_ge(s["xnt_ps"], half_no(b, h) + 1)
                nc.scalar.copy(xnt_hi[:], BANK["spread1", h][:]).then_inc(s["xnt_hi_set"], 1)

            def hidden(b, h):
                act.wait_ge(s["hid_ps"], half_no(b, h) + 1)
                nc.scalar.activation(hid[:], BANK["hidden", h][:], ACT.Tanh, bias=b1_col[:, 0:1]).then_inc(s["hid_set"], 1)

            def weigh(b, h):
                n = half_no(b, h)
                act.wait_ge(s["weight_set"], b + 1)
                wait(act, "xwt_ps", n)
                for t in range(TILES):
                    last = nc.scalar.activation(xw[:, t, :], xn[h][:, t, :], ACT.Copy,
                                                scale=weight[:, h * TILES + t:h * TILES + t + 1])
                last.then_inc(s["xw_set"], 1)

            def norm2(b, h):
                n = half_no(b, h)
                act.wait_ge(s["scale2_set"], n + 1)
                wait(act, "xft_ps", n)
                for t in range(TILES):
                    last = nc.scalar.activation(xf[:, t, :], x_att[h][:, t, :], ACT.Identity,
                                                bias=shift2[h][:, t:t + 1], scale=rstd2[h][:, t:t + 1])
                last.then_inc(s["xf_set"], 1)

            def spread2(b, h):
                act.wait_ge(s["xft_ps"], half_no(b, h) + 1)
                nc.scalar.copy(xft_hi[h][:], BANK["spread2", h][:]).then_inc(s["xft_hi_set"], 1)

            def logits(b, h):
                act.wait_ge(s["logit_ps"], half_no(b, h) + 1)
                nc.scalar.copy(logit_t[:], BANK["logits", h][0:E, :]).then_inc(s["logit_set"], 1)

            def gates(b, h):
                n = half_no(b, h)
                act.wait_ge(s["logit_cols_ps"], n + 1)
                act.wait_ge(s["half_inv_set"], n + 1)
                wait(act, "comb_set", n)
                for t in range(TILES):
                    last = nc.scalar.activation(tanh_half[:, t, :], BANK["gates", h][:, t * E:(t + 1) * E],
                                                ACT.Tanh, scale=half_inv[h][:, t:t + 1])
                last.then_inc(s["tanh_set"], 1)

            def route(b, h):
                act.wait_ge(s["comb_ps"], half_no(b, h) + 1)
                nc.scalar.copy(comb_t[h][:], BANK["route", h][0:2 * E, :]).then_inc(s["comb_t_set"], 1)

            def hidden_high(b, h, i):
                if i == 0:
                    act.wait_ge(s["prod_set"], chunk_no(b, h, 1))
                    last = nc.scalar.copy(h_shared[0:H, :], hfull[(CHUNKS * h) % 2][0:H, :])
                else:
                    act.wait_ge(s["hfull_set"], PAIRS * half_no(b, h) + i)
                    last = nc.scalar.copy(h_hi[i % 3][:], hfull[(CHUNKS * h + i) % 2][:])
                last.then_inc(s["h_hi_set"], 1)

            def before(b, h, i):
                return (b, h, i - 1) if i else ((b, 0, CHUNKS - 1) if h else (b - 1, 1, CHUNKS - 1))

            def score_stage(b, h):
                act.wait_ge(s["score_ps"], half_no(b, h) + 1)
                if h == 0:
                    wait(act, "score_cols_ps", b)
                nc.scalar.activation(score_row[h][:], BANK["score", h][0:1, :], ACT.Identity,
                                     bias=b2_sb[0:1, 0:1]).then_inc(s["score_row_set"], 1)

            def step(b, h, i, between):
                c = chunk_no(b, h, i)
                act.wait_ge(s["gate_ready"], c + 1)
                wait(act, "prod_set", c - 1)
                rows = slice(0, H if i == 0 else P)
                buf = (CHUNKS * h + i) % 2
                nc.scalar.activation(silu[buf][rows, :], ps_gate[buf][rows, :], ACT.Silu).then_inc(s["silu_set"], 1)
                if not (isinstance(c, int) and c == 0):
                    hidden_high(*before(b, h, i))
                between()

            def collect(b, h):
                act.wait_ge(s["down_done"], chunk_no(b, h, CHUNKS))
                nc.scalar.copy(y_t[:], ps_y[:]).then_inc(s["y_set"], 1)

            run("act", step, {
                       "shared_weights": shared_weights, "gate_weights": gate_weights, "up_weights": up_weights,
                       "down_weights": down_weights, "score": score_stage, "norm1": norm1, "spread1": spread1, "hidden": hidden,
                       "weigh": weigh, "norm2": norm2, "spread2": spread2, "logits": logits, "gates": gates,
                       "route": route, "collect": collect}, act)
            hidden_high(B - 1, 1, CHUNKS - 1)
            collect(B - 1, 1)

        @block.gpsimd
        def _(pool):
            nc.gpsimd.memset(euler[:], 2.718281828459045).then_inc(s["consts_set"], 1)
            nc.gpsimd.memset(minus_half[:], -0.5).then_inc(s["consts_set"], 1)
            nc.gpsimd.memset(ones[:], 1.0).then_inc(s["consts_set"], 1)
            nc.gpsimd.memset(zeros[:], 0.0).then_inc(s["consts_set"], 1)
            nc.gpsimd.memset(tile_sums[:, 0:1], 0.0).then_inc(s["consts_set"], 1)
            nc.gpsimd.memset(gwt[:], 0.0).then_inc(s["gwt_zeroed"], 1)
            pool.wait_ge(s["consts_set"], 5)

            def small_weights(b, h):
                pool.wait_ge(s["gw_squared"], 2)
                nc.gpsimd.tensor_tensor(gw_inv[:], gw_n2[:], minus_half[0:E, 0:1], ALU.pow).then_inc(s["gw_scaled"], 1)

            def stats1(b, h):
                n = half_no(b, h)
                pool.wait_ge(s["stats1_set"], n + 1)
                nc.gpsimd.tensor_tensor(rstd1[h][:], var_eps1[h][:], minus_half[:], ALU.pow).then_inc(s["scale1_pool"], 1)
                pool.wait_ge(s["scale1_pool"], n + 1)
                nc.gpsimd.tensor_tensor(shift1[h][:], neg_mean1[h][:], rstd1[h][:], ALU.mult).then_inc(s["scale1_set"], 1)

            def softmax(b, h):
                pool.wait_ge(s["top_set"], b + 1)
                nc.gpsimd.tensor_tensor(own_score[:], score[:], zeros[:, 0:2 * TILES], ALU.add)
                nc.gpsimd.partition_all_reduce(top_all[:], top[:], P, bass.bass_isa.ReduceOp.max).then_inc(s["weight_pool"], 1)
                pool.wait_ge(s["weight_pool"], 2 * b + 1)
                nc.gpsimd.tensor_tensor(below[:], own_score[:], top_all[:].broadcast_to([P, 2 * TILES]),
                                        ALU.subtract).then_inc(s["weight_pool"], 1)
                pool.wait_ge(s["weight_pool"], 2 * b + 2)
                wait(pool, "xw_set", 2 * b)
                nc.gpsimd.tensor_tensor(weight[:], euler[:], below[:], ALU.pow).then_inc(s["weight_set"], 1)

            def attend(b, h):
                n = half_no(b, h)
                pool.wait_ge(s["stats2_set"], n + 1)
                nc.gpsimd.tensor_tensor(rstd2[h][:], var_eps2[h][:], minus_half[:], ALU.pow).then_inc(s["scale2_pool"], 1)
                pool.wait_ge(s["scale2_pool"], 4 * n + 1)
                nc.gpsimd.tensor_tensor(xf_norm[h][:], var512[h][:], rstd2[h][:], ALU.mult).then_inc(s["scale2_pool"], 1)
                pool.wait_ge(s["scale2_pool"], 4 * n + 2)
                nc.gpsimd.tensor_tensor(xf_norm2[h][:], xf_norm[h][:], rstd2[h][:], ALU.mult).then_inc(s["scale2_pool"], 1)
                pool.wait_ge(s["scale2_pool"], 4 * n + 3)
                nc.gpsimd.tensor_tensor(shift2[h][:], neg_mean2[h][:], rstd2[h][:], ALU.mult).then_inc(s["scale2_set"], 1)
                nc.gpsimd.tensor_scalar(xf_norm3[h][:], xf_norm2[h][:], 4 * NORM_EPS ** 2, None, ALU.max).then_inc(s["scale2_pool"], 1)
                pool.wait_ge(s["scale2_pool"], 4 * n + 4)
                nc.gpsimd.tensor_tensor(half_inv[h][:], xf_norm3[h][:], minus_half[:], ALU.pow).then_inc(s["half_inv_set"], 1)

            def hidden_low(b, h, i):
                if i == 0:
                    return
                pool.wait_ge(s["h_hi_set"], chunk_no(b, h, i) + 1)
                nc.gpsimd.tensor_tensor(h_lo[i % 3][:], hfull[(CHUNKS * h + i) % 2][:], word(h_hi[i % 3][:]),
                                        ALU.subtract).then_inc(s["h_lo_set"], 1)

            def step(b, h, i, between):
                if i:
                    hidden_low(b, h, i - 1)
                elif not (isinstance(b, int) and b == 0 and h == 0):
                    hidden_low(*((b, 0) if h else (b - 1, 1)), CHUNKS - 1)
                between()

            run("pool", step, {"small_weights": small_weights, "stats1": stats1, "softmax": softmax, "attend": attend}, pool)
            hidden_low(B - 1, 1, CHUNKS - 1)

        @block.vector
        def _(dve):
            def low(out_, whole, hi, name):
                return nc.vector.tensor_tensor(out_, whole, word(hi), ALU.subtract).then_inc(s[name], 1)

            def small_weights(b, h):
                dve.wait_ge(s["gwt_in"], 16)
                nc.vector.scalar_tensor_tensor(out=gw_sq[:], in0=gw_sb[:], scalar=1.0, in1=gw_sb[:], op0=ALU.mult,
                                               op1=ALU.mult).then_inc(s["gw_squared"], 1)
                dve.wait_ge(s["gw_squared"], 1)
                nc.vector.tensor_reduce(gw_inv[:], gw_sq[:], AX.X, ALU.add).then_inc(s["gw_unit_set"], 1)
                dve.wait_ge(s["gw_unit_set"], 1)
                nc.vector.tensor_scalar(gw_n2[:], gw_inv[:], NORM_EPS ** 2, None, ALU.max).then_inc(s["gw_squared"], 1)
                dve.wait_ge(s["w1t_ps"], 1)
                nc.vector.tensor_copy(w1t[:], ps_a[:, 0:P]).then_inc(s["w1t_split"], 1)
                dve.wait_ge(s["w1t_split"], 1)
                nc.vector.tensor_copy(w1t_hi[:], w1t[:]).then_inc(s["w1t_split"], 1)
                dve.wait_ge(s["w1t_split"], 2)
                low(w1t_lo[:], w1t[:], w1t_hi[:], "w1t_split")
                dve.wait_ge(s["gw_scaled"], 1)
                nc.vector.tensor_scalar(gw_unit[:], gw_sb[:], gw_inv[:, 0:1], None, ALU.mult).then_inc(s["gw_unit_set"], 1)
                dve.wait_ge(s["gwt_zeroed"], 1)
                dve.wait_ge(s["gwt_ps"], 1)
                nc.vector.tensor_copy(gwt[:, 0:E], ps_b[:, 0:E]).then_inc(s["gwt_split"], 1)
                dve.wait_ge(s["gwt_split"], 1)
                nc.vector.tensor_copy(gwt_hi[:], gwt[:]).then_inc(s["gwt_split"], 1)
                dve.wait_ge(s["gwt_split"], 2)
                low(gwt_lo[:], gwt[:], gwt_hi[:], "gwt_split")

            def shared_weights(b, h):
                dve.wait_ge(s["shared_hi"], 1)
                low(gu_lo[:, 0:2 * H], gu_sb[:, 0:2 * H], gu_hi[:, 0:2 * H], "shared_lo")

            def gate_weights(b, h):
                dve.wait_ge(s["gu_hi_set"], 1)
                low(gu_lo[:, GATE], gu_sb[:, GATE], gu_hi[:, GATE], "gu_lo_set")

            def up_weights(b, h):
                dve.wait_ge(s["gu_hi_set"], 2)
                low(gu_lo[:, UP], gu_sb[:, UP], gu_hi[:, UP], "gu_lo_set")

            def down_weights(b, h):
                dve.wait_ge(s["dn_hi_set"], 1)
                low(dn_lo[:], dn_sb[:], dn_hi[:], "dn_lo_set")

            def moments(src, bn, mv, chain, n):
                for t in range(TILES):
                    last = nc.vector.bn_stats(bn[:, t, :], src[:, t, :])
                dve.drain()
                for t in range(TILES):
                    last = nc.vector.bn_aggr(mv[:, t, :], bn[:, t, :])
                last.then_inc(s[chain], 1)
                dve.wait_ge(s[chain], n + 1)

            def stats1(b, h):
                n = half_no(b, h)
                dve.wait_ge(x_in_loaded[h], 16 * b + 16)
                wait(dve, "xn_set", n - 1)
                moments(x_in[h], bn1[h], mv1[h], "stats1_dve", n)
                nc.vector.tensor_scalar(neg_mean1[h][:], mv1[h][:, :, 0], -1.0, None, ALU.mult)
                nc.vector.tensor_scalar(var_eps1[h][:], mv1[h][:, :, 1], EPS, None, ALU.add).then_inc(s["stats1_set"], 1)

            def spread1(b, h):
                dve.wait_ge(s["xnt_hi_set"], half_no(b, h) + 1)
                low(xnt_lo[:], BANK["spread1", h][:], xnt_hi[:], "xnt_lo_set")

            def softmax(b, h):
                dve.wait_ge(s["score_cols_ps"], b + 1)
                wait(dve, "weight_set", b)
                nc.vector.tensor_copy(score[:], BANK["softmax", 0][:, 0:2 * TILES]).then_inc(s["score_dve"], 1)
                dve.wait_ge(s["score_dve"], b + 1)
                nc.vector.tensor_reduce(top[:], score[:], AX.X, ALU.max).then_inc(s["top_set"], 1)

            def sums(b, h):
                dve.wait_ge(s["weight_set"], b + 1)
                nc.vector.tensor_tensor_scan(tile_sums[:, 1:2 * TILES + 1], weight[:], zeros[:, 0:2 * TILES],
                                             0.0, ALU.add, ALU.add).then_inc(s["sums_set"], 1)

            def denominator(b, h):
                dve.wait_ge(s["den_ps"], b + 1)
                nc.vector.reciprocal(inv_den[:], BANK["denominator", 0][:, 0:2 * TILES]).then_inc(s["inv_den_set"], 1)

            def scan(b, h):
                n = half_no(b, h)
                dve.wait_ge(s["xwt_ps"], n + 1)
                if h == 1:
                    dve.wait_ge(s["num_set"], n)
                wait(dve, "num_ps", n - 1)
                start = num_t[0][:, HALF - 1:HALF] if h else 0.0
                nc.vector.tensor_tensor_scan(num_t[h][:], zeros[:], BANK["scan", h][:], start, ALU.add,
                                             ALU.add).then_inc(s["num_set"], 1)

            def attend(b, h):
                n = half_no(b, h)
                dve.wait_ge(s["num_ps"], n + 1)
                dve.wait_ge(s["inv_den_set"], b + 1)
                dve.wait_ge(x_raw_loaded[h], 16 * b + 16)
                for t in range(TILES):
                    col = h * TILES + t
                    last = nc.vector.scalar_tensor_tensor(
                        out=x_att[h][:, t, :], in0=BANK["attend", h][:, tile(t)], scalar=inv_den[:, col:col + 1],
                        in1=x_raw[h][:, t, :], op0=ALU.mult, op1=ALU.add)
                last.then_inc(s["attended"], 1)
                dve.wait_ge(s["attended"], n + 1)
                moments(x_att[h], bn2[h], mv2[h], "stats2_dve", n)
                nc.vector.tensor_scalar(neg_mean2[h][:], mv2[h][:, :, 0], -1.0, None, ALU.mult)
                nc.vector.tensor_scalar(var512[h][:], mv2[h][:, :, 1], 4.0 * D, None, ALU.mult)
                nc.vector.tensor_scalar(var_eps2[h][:], mv2[h][:, :, 1], EPS, None, ALU.add).then_inc(s["stats2_set"], 1)

            def spread2(b, h):
                dve.wait_ge(s["xft_hi_set"], half_no(b, h) + 1)
                low(xft_lo[h][:], BANK["spread2", h][:], xft_hi[h][:], "xft_lo_set")

            def gates(b, h):
                n = half_no(b, h)
                chain = [0]

                def link(ins):
                    ins.then_inc(s["route_dve"], 1)
                    chain[0] += 1
                    dve.wait_ge(s["route_dve"], 5 * n + chain[0])

                dve.wait_ge(s["tanh_set"], n + 1)
                nc.vector.tensor_scalar(gate[:], tanh_half[:], 0.5, 0.5, ALU.mult, ALU.add)
                dve.drain()
                for t in range(TILES):
                    nc.vector.max(best[:, t, :], gate[:, t, :])
                dve.drain()
                for t in range(TILES):
                    last = nc.vector.match_replace(struck[:, t, :], best[:, t, :], gate[:, t, :], -1.0)
                link(last)
                nc.vector.scalar_tensor_tensor(out=chosen[:], in0=struck[:], scalar=0.0, in1=gate[:],
                                               op0=ALU.is_lt, op1=ALU.mult)
                link(nc.vector.tensor_reduce(best_sum[:], best[:], AX.X, ALU.add))
                link(nc.vector.reciprocal(inv_best[:], best_sum[:]))
                link(nc.vector.tensor_tensor(comb[:], chosen[:], inv_best[:].unsqueeze(2).broadcast_to([P, TILES, E]),
                                             ALU.mult))
                wait(dve, "comb_ps", n)
                link(nc.vector.tensor_copy(comb_hl[:, :, 0:E], comb[:]))
                nc.vector.tensor_tensor(comb_hl[:, :, E:2 * E], comb[:], word(comb_hl[:, :, 0:E]),
                                        ALU.subtract).then_inc(s["comb_set"], 1)

            def step(b, h, i, between):
                chunk(b, h, i)
                between()

            def chunk(b, h, i):
                c = chunk_no(b, h, i)
                n = half_no(b, h)
                buf = (CHUNKS * h + i) % 2
                dve.wait_ge(s["silu_set"], c + 1)
                if i == 0:
                    wait(dve, "h_lo_set", PAIRS * n - 1)
                    nc.vector.tensor_tensor(hfull[buf][0:H, :], silu[buf][0:H, :], ps_gate[buf][H:P, :],
                                            ALU.mult).then_inc(s["prod_set"], 1)
                    return
                dve.wait_ge(s["up_ready"], PAIRS * n + i)
                nc.vector.tensor_tensor(prod[buf][:], silu[buf][:], ps_up[buf][:], ALU.mult).then_inc(s["prod_set"], 1)
                dve.wait_ge(s["comb_ready"], PAIRS * n + i)
                dve.wait_ge(s["prod_set"], c + 1)
                if i == 2:
                    dve.wait_ge(s["shared_lo_set"], n + 1)
                elif i == 1:
                    wait(dve, "h_lo_set", PAIRS * n)
                else:
                    dve.wait_ge(s["h_lo_set"], PAIRS * n + i - 2)
                nc.vector.tensor_tensor(hfull[buf][:], prod[buf][:], ps_comb[:], ALU.mult).then_inc(s["hfull_set"], 1)
                if i == 1:
                    dve.wait_ge(s["h_hi_set"], chunk_no(b, h, 1))
                    low(h_shared[H:P, :], hfull[1 - buf][0:H, :], h_shared[0:H, :], "shared_lo_set")

            def out_stage(b, h):
                dve.wait_ge(s["out_ps"], half_no(b, h) + 1)
                dve.wait_ge(stored[h], 16 * b + 16)
                nc.vector.tensor_tensor(result[h][:].rearrange("p t d -> p (t d)"), BANK["out", h][:],
                                        x_att[h][:].rearrange("p t d -> p (t d)"), ALU.add).then_inc(s["result_set"], 1)

            for h in range(2):
                nc.vector.memset(result[h][:, 0, 0:1], 0.0).then_inc(stored[h], 16)
            run("dve", step, {
                       "small_weights": small_weights, "shared_weights": shared_weights,
                       "gate_weights": gate_weights, "up_weights": up_weights, "down_weights": down_weights,
                       "stats1": stats1, "spread1": spread1, "softmax": softmax, "sums": sums,
                       "denominator": denominator, "scan": scan, "attend": attend, "spread2": spread2,
                       "gates": gates, "out": out_stage}, dve)
            out_stage(B - 1, 1)

        @block.tensor
        def _(pe):
            mm = nc.tensor.matmul

            def split_product(out_, w_hi, w_lo, m_hi, m_lo, start=True, stop=True):
                mm(out_, w_hi, m_lo, start=start, stop=False)
                mm(out_, w_lo, m_hi, start=False, stop=False)
                return mm(out_, w_hi, m_hi, start=False, stop=stop)

            def transposes(out_, src):
                for t in range(TILES):
                    last = nc.tensor.transpose(out_[:, tile(t)], src(t), ident[:])
                return last

            def turn(t, out_, src, eye):
                if t == 0:
                    return mm(out_, src, eye, start=True, stop=True)
                return nc.tensor.transpose(out_, src, eye)

            def is_int(b, value):
                return isinstance(b, int) and b == value

            def small_weights(b, h):
                pe.wait_ge(s["ident_in"], 16)
                pe.wait_ge(s["small_in"], 16 * 5)
                nc.tensor.transpose(ps_a[:, 0:P], w1_sb[:], ident[:]).then_inc(s["w1t_ps"], 1)
                pe.wait_ge(s["gw_unit_set"], 2)
                nc.tensor.transpose(ps_b[:, 0:E], gw_unit[:], ident[0:E, 0:E]).then_inc(s["gwt_ps"], 1)

            def spread1(b, h):
                pe.wait_ge(s["xn_set"], half_no(b, h) + 1)
                if is_int(b, 0):
                    pe.wait_ge(s["w1t_split" if h else "gwt_split"], 1)
                transposes(BANK["spread1", h], lambda t: xn[h][:, t, :]).then_inc(s["xnt_ps"], 1)

            def hidden(b, h):
                pe.wait_ge(s["xnt_lo_set"], half_no(b, h) + 1)
                if is_int(b, 0) and h == 0:
                    pe.wait_ge(s["w1t_split"], 3)
                split_product(BANK["hidden", h][:], w1t_hi[:], w1t_lo[:], xnt_hi[:],
                              xnt_lo[:]).then_inc(s["hid_ps"], 1)

            def score_stage(b, h):
                pe.wait_ge(s["hid_set"], half_no(b, h) + 1)
                mm(BANK["score", h][0:1, :], w2_col[:], hid[:], start=True, stop=True).then_inc(s["score_ps"], 1)

            def softmax(b, h):
                pe.wait_ge(s["score_row_set"], 2 * b + 2)
                for t in range(2 * TILES):
                    last = turn(t, BANK["softmax", 0][:, t:t + 1], score_row[t // TILES][:, tile(t % TILES)],
                                ident[0:1, 0:1])
                last.then_inc(s["score_cols_ps"], 1)

            def scan(b, h):
                pe.wait_ge(s["xw_set"], half_no(b, h) + 1)
                if h == 0:
                    pe.wait_ge(s["inv_den_set"], b + 1)
                transposes(BANK["scan", h], lambda t: xw[:, t, :]).then_inc(s["xwt_ps"], 1)

            def denominator(b, h):
                pe.wait_ge(s["sums_set"], b + 1)
                den = BANK["denominator", 0][:, 0:2 * TILES]
                mm(den, ones[:], tile_sums[:, 0:2 * TILES], start=True, stop=False)
                mm(den, upto_sb[:], weight[:], start=False, stop=True).then_inc(s["den_ps"], 1)

            def attend(b, h):
                pe.wait_ge(s["num_set"], half_no(b, h) + 1)
                transposes(BANK["attend", h], lambda t: num_t[h][:, tile(t)]).then_inc(s["num_ps"], 1)

            def spread2(b, h):
                pe.wait_ge(s["xf_set"], half_no(b, h) + 1)
                transposes(BANK["spread2", h], lambda t: xf[:, t, :]).then_inc(s["xft_ps"], 1)

            def logits(b, h):
                pe.wait_ge(s["xft_lo_set"], half_no(b, h) + 1)
                if is_int(b, 0) and h == 0:
                    pe.wait_ge(s["gwt_split"], 3)
                split_product(BANK["logits", h][:], gwt_hi[:], gwt_lo[:], xft_hi[h][:],
                              xft_lo[h][:]).then_inc(s["logit_ps"], 1)

            def gates(b, h):
                pe.wait_ge(s["logit_set"], half_no(b, h) + 1)
                for t in range(TILES):
                    last = turn(t, BANK["gates", h][:, t * E:(t + 1) * E], logit_t[:, tile(t)], ident[0:E, 0:E])
                last.then_inc(s["logit_cols_ps"], 1)

            def route(b, h):
                pe.wait_ge(s["comb_set"], half_no(b, h) + 1)
                for t in range(TILES):
                    last = nc.tensor.transpose(BANK["route", h][0:2 * E, tile(t)], word(comb_hl[:, t, :]), ident[:])
                last.then_inc(s["comb_ps"], 1)

            def out_stage(b, h):
                pe.wait_ge(s["y_set"], half_no(b, h) + 1)
                if h and not (isinstance(b, int) and b + 2 >= B):
                    pe.wait_ge(s["score_row_set"], 2 * (b + 2) + 1)
                transposes(BANK["out", h], lambda t: y_t[:, tile(t)]).then_inc(s["out_ps"], 1)

            def down(b, h, i):
                n = half_no(b, h)
                cols = slice(i * D, (i + 1) * D)
                pe.wait_ge(s["h_hi_set"], chunk_no(b, h, i) + 1)
                if i == 0:
                    pe.wait_ge(s["shared_lo_set"], n + 1)
                    wait(pe, "y_set", n)
                    if is_int(b, 0) and h == 0:
                        pe.wait_ge(s["dn_lo_set"], 1)
                    mm(ps_y[:], dn_lo[:, cols], h_shared[:], start=True, stop=False)
                    last = mm(ps_y[:], dn_hi[:, cols], h_shared[:], start=False, stop=False)
                else:
                    pe.wait_ge(s["h_lo_set"], PAIRS * n + i)
                    last = split_product(ps_y[:], dn_hi[:, cols], dn_lo[:, cols], h_hi[i % 3][:], h_lo[i % 3][:],
                                         start=False, stop=i == CHUNKS - 1)
                last.then_inc(s["down_done"], 1)

            def step(b, h, i, between):
                c = chunk_no(b, h, i)
                n = half_no(b, h)
                buf = (CHUNKS * h + i) % 2
                if i == 0:
                    pe.wait_ge(s["xft_lo_set"], n + 1)
                    if is_int(b, 0) and h == 0:
                        pe.wait_ge(s["shared_lo"], 1)
                if i == 1 and is_int(b, 0) and h == 0:
                    pe.wait_ge(s["gu_lo_set"], 2)
                    pe.wait_ge(s["select_set"], 1)
                wait(pe, "prod_set", c - 1)

                def from_x(bank, first):
                    cols = slice(first, first + P)
                    return split_product(bank[:], gu_hi[:, cols], gu_lo[:, cols], xft_hi[h][:], xft_lo[h][:])

                if i == 0:
                    from_x(ps_gate[buf], 0).then_inc(s["gate_ready"], 1)
                else:
                    from_x(ps_gate[buf], GATE.start + (i - 1) * P).then_inc(s["gate_ready"], 1)
                    from_x(ps_up[buf], UP.start + (i - 1) * P).then_inc(s["up_ready"], 1)
                between()
                if i:
                    if i == 1:
                        pe.wait_ge(s["comb_t_set"], n + 1)
                    wait(pe, "hfull_set", PAIRS * n + i - 1)
                    mm(ps_comb[:], select[:, (i - 1) * P:i * P], comb_t[h][:], start=True,
                       stop=True).then_inc(s["comb_ready"], 1)
                if i >= LAG:
                    down(b, h, i - LAG)
                elif h:
                    down(b, 0, CHUNKS + i - LAG)
                elif not is_int(b, 0):
                    down(b - 1, 1, CHUNKS + i - LAG)

            run("pe", step, {
                       "small_weights": small_weights, "spread1": spread1, "hidden": hidden, "score": score_stage,
                       "softmax": softmax, "scan": scan, "denominator": denominator, "attend": attend,
                       "spread2": spread2, "logits": logits, "gates": gates, "route": route, "out": out_stage},
                pe)
            for i in range(CHUNKS - LAG, CHUNKS):
                down(B - 1, 1, i)
            out_stage(B - 1, 1)


_INS = ["L0_attn_x", "L0_attn_W1", "L0_attn_b1_", "L0_attn_W2", "L0_attn_b2_", "L0_ffn_gate_w", "L0_ffn_w_gate",
        "L0_ffn_w_up", "L0_ffn_w_down", "L0_ffn_sw_gate", "L0_ffn_sw_up", "L0_ffn_sw_down"]


def kernel(**inputs):
    import numpy as np
    import concourse.bacc as bacc
    from concourse.bass_utils import run_bass_kernel_spmd

    arrays = {f"in_{name}": np.ascontiguousarray(inputs[name]) for name in _INS}
    arrays["identity"] = np.eye(P, dtype=np.float32)
    arrays["pair_select"] = np.tile(np.kron(np.eye(E, dtype=np.float32), np.ones((1, H), np.float32)), (2, 1))
    arrays["upto"] = np.triu(np.ones((P, P), np.float32))
    nc = bacc.Bacc("TRN2", target_bir_lowering=False, num_devices=1)
    args = [nc.dram_tensor(name, a.shape, mybir.dt.from_np(a.dtype), kind="ExternalInput").ap()
            for name, a in arrays.items()]
    result = nc.dram_tensor("out_dram", (B, T, D), mybir.dt.float32, kind="ExternalOutput").ap()
    attention_moe_kernel(nc, *args, result)
    r = run_bass_kernel_spmd(nc, [arrays], core_ids=[0])
    return r.results[0]["out_dram"]
```

```python
import concourse.bass as bass
from concourse import mybir
from contextlib import ExitStack

B, T, D = 4, 1024, 128
E, H, K = 16, 64, 8
P = 128
HALF = T // 2
TILES = HALF // P
PAIRS = E // 2
CHUNKS = 1 + PAIRS
STEPS = 2 * CHUNKS
LAG = 3
EPS = 1e-5
NORM_EPS = 1e-12
GU = 2 * H + 2 * E * H
GATE = slice(2 * H, 2 * H + E * H)
UP = slice(2 * H + E * H, GU)

STAGES = {
    "pe": {
        0: [("score", 1, 0), ("spread2", 0, 1)],
        1: [("route", 0, 0), ("logits", 0, 1)],
        2: [("gates", 0, 1), ("spread1", 1, 1)],
        4: [("out", -1, 1), ("hidden", 1, 1)],
        5: [("score", 1, 1), ("softmax", 1, 0)],
        7: [("route", 0, 1)],
        8: [("denominator", 1, 0)],
        9: [("scan", 1, 0)],
        10: [("attend", 1, 0)],
        11: [("scan", 1, 1)],
        12: [("out", 0, 0)],
        14: [("attend", 1, 1), ("spread2", 1, 0)],
        15: [("logits", 1, 0), ("spread1", 2, 0)],
        16: [("gates", 1, 0)],
        17: [("hidden", 2, 0)],
    },
    "dve": {
        0: [("stats1", 1, 1), ("spread2", 0, 1)],
        2: [("spread1", 1, 1)],
        3: [("choose", 0, 1), ("out", -1, 1), ("share", 0, 1)],
        4: [("softmax", 1, 0)],
        5: [("sums", 1, 0)],
        7: [("denominator", 1, 0)],
        8: [("scan", 1, 0)],
        9: [("attend", 1, 0)],
        11: [("stats2", 1, 0), ("scan", 1, 1)],
        12: [("stats1", 2, 0), ("out", 0, 0)],
        13: [("attend", 1, 1)],
        14: [("spread2", 1, 0), ("stats2", 1, 1)],
        15: [("spread1", 2, 0)],
        16: [("choose", 1, 0)],
        17: [("share", 1, 0)],
    },
    "act": {
        0: [("score", 1, 0), ("spread2", 0, 1), ("route", 0, 0)],
        1: [("logits", 0, 1), ("norm1", 1, 1)],
        2: [("collect", -1, 1)],
        3: [("spread1", 1, 1), ("gates", 0, 1)],
        4: [("hidden", 1, 1), ("score", 1, 1)],
        6: [("weigh", 1, 0)],
        7: [("route", 0, 1)],
        9: [("weigh", 1, 1)],
        11: [("collect", 0, 0)],
        13: [("norm2", 1, 0)],
        14: [("spread2", 1, 0), ("norm1", 2, 0)],
        15: [("spread1", 2, 0), ("logits", 1, 0)],
        16: [("gates", 1, 0), ("norm2", 1, 1)],
        17: [("hidden", 2, 0)],
    },
    "pool": {
        1: [("stats1", 1, 1)],
        4: [("softmax", 1, 0), ("powers", 1, 0)],
        8: [("keep", 0, 1)],
        11: [("scale2", 1, 0)],
        12: [("norms", 1, 0), ("stats1", 2, 0), ("keep", 1, 0)],
        14: [("scale2", 1, 1)],
        15: [("norms", 1, 1)],
    },
}
FIRST_STAGES = [
    [("stats1", 0, 0), ("hidden_weights", 0, 0), ("norm1", 0, 0), ("stats1", 0, 1), ("norm1", 0, 1),
     ("spread1", 0, 0), ("shared_weights", 0, 0), ("spread1", 0, 1), ("hidden", 0, 0), ("hidden", 0, 1),
     ("down_weights", 0, 0), ("score", 0, 0), ("score", 0, 1), ("router_weights", 0, 0), ("softmax", 0, 0),
     ("down_low", 0, 0), ("powers", 0, 0), ("scale2", 0, 0), ("gate_weights", 0, 0), ("gate_low", 0, 0),
     ("sums", 0, 0), ("denominator", 0, 0), ("up_low", 0, 0), ("up_weights", 0, 0), ("scan", 0, 0),
     ("attend", 0, 0), ("weigh", 0, 0), ("stats2", 0, 0), ("weigh", 0, 1), ("norm2", 0, 0), ("scan", 0, 1),
     ("stats1", 1, 0), ("norms", 0, 0), ("norm1", 1, 0), ("attend", 0, 1), ("spread2", 0, 0), ("stats2", 0, 1)],
    [("spread1", 1, 0), ("logits", 0, 0), ("hidden", 1, 0), ("scale2", 0, 1), ("gates", 0, 0), ("norm2", 0, 1),
     ("choose", 0, 0), ("share", 0, 0), ("norms", 0, 1), ("keep", 0, 0)],
]
BANKS = {
    "spread1": "bb", "hidden": "bb", "score": "ab", "softmax": "b", "denominator": "a", "scan": "bb",
    "attend": "bb", "spread2": "ab", "logits": "ab", "gates": "aa", "route": "aa", "out": "aa",
}
HEAD = 5
AHEAD = 2


def attention_moe_kernel(nc: bass.Bass, x, w1, b1, w2, b2, gate_w, w_gate, w_up, w_down,
                         sw_gate, sw_up, sw_down, identity, pair_select, upto, out):
    f32 = mybir.dt.float32
    f32r = mybir.dt.float32r
    ALU = mybir.AluOpType
    ACT = mybir.ActivationFunctionType
    AX = mybir.AxisListType

    ctx = ExitStack()
    with ctx:
        def sb(name, shape, dt=f32):
            return ctx.enter_context(nc.sbuf_tensor(name, shape, dt))

        def pb(name):
            return ctx.enter_context(nc.psum_tensor(name, [P, HALF], f32))

        def sem(name):
            return ctx.enter_context(nc.semaphore(name))

        def word(ap):
            return ap.bitcast(f32)

        ident = sb("ident", [P, P])
        upto_sb = sb("upto_sb", [P, P])
        ones = sb("ones", [P, P])
        select_f = sb("select_f", [2 * E, PAIRS * P])
        select = sb("select", [2 * E, PAIRS * P], f32r)
        w1_sb = sb("w1_sb", [P, D])
        w1t = sb("w1t", [P, P])
        w1t_hi, w1t_lo = sb("w1t_hi", [P, P], f32r), sb("w1t_lo", [P, P], f32r)
        w2_col = sb("w2_col", [P, 1])
        b1_col = sb("b1_col", [P, 1])
        b2_sb = sb("b2_sb", [1, 1])
        gw_sb = sb("gw_sb", [E, D])
        gw_sq = sb("gw_sq", [E, D])
        gw_n2 = sb("gw_n2", [E, 1])
        gw_inv = sb("gw_inv", [E, 1])
        gw_unit = sb("gw_unit", [E, D])
        gwt = sb("gwt", [P, P])
        gwt_hi, gwt_lo = sb("gwt_hi", [P, P], f32r), sb("gwt_lo", [P, P], f32r)
        gu_sb = sb("gu_sb", [P, GU])
        gu_hi, gu_lo = sb("gu_hi", [P, GU], f32r), sb("gu_lo", [P, GU], f32r)
        dn_sb = sb("dn_sb", [P, CHUNKS * D])
        dn_hi, dn_lo = sb("dn_hi", [P, CHUNKS * D], f32r), sb("dn_lo", [P, CHUNKS * D], f32r)
        euler = sb("euler", [P, 2 * TILES])
        minus_half = sb("minus_half", [P, TILES])
        zeros = sb("zeros", [P, HALF])
        started = sb("started", [P, 3])
        first_silu = sb("first_silu", [1, 1])

        def pair(name, shape, dt=f32):
            return [sb(f"{name}{h}", shape, dt) for h in range(2)]

        x_in = pair("x_in", [P, TILES, D])
        x_raw = pair("x_raw", [P, TILES, D])
        x_att = pair("x_att", [P, TILES, D])
        xn = pair("xn", [P, TILES, D])
        bn1, bn2 = pair("bn1_", [P, TILES, 6]), pair("bn2_", [P, TILES, 6])
        mv1, mv2 = pair("mv1_", [P, TILES, 2]), pair("mv2_", [P, TILES, 2])
        var_eps1, var_eps2 = pair("var_eps1_", [P, TILES]), pair("var_eps2_", [P, TILES])
        neg_mean1, neg_mean2 = pair("neg_mean1_", [P, TILES]), pair("neg_mean2_", [P, TILES])
        rstd1, rstd2 = pair("rstd1_", [P, TILES]), pair("rstd2_", [P, TILES])
        shift1, shift2 = pair("shift1_", [P, TILES]), pair("shift2_", [P, TILES])
        var512 = pair("var512_", [P, TILES])
        xf_norm = pair("xf_norm", [P, TILES])
        xf_norm2 = pair("xf_norm2_", [P, TILES])
        xf_norm3 = pair("xf_norm3_", [P, TILES])
        half_inv = pair("half_inv", [P, TILES])
        xnt_hi, xnt_lo = pair("xnt_hi", [P, HALF], f32r), pair("xnt_lo", [P, HALF], f32r)
        hid = pair("hid", [P, HALF])
        score_row = pair("score_row", [1, HALF])
        score = sb("score", [P, 2 * TILES])
        top = sb("top", [P, 1])
        own_score = sb("own_score", [P, 2 * TILES])
        top_all = sb("top_all", [P, 1])
        below = sb("below", [P, 2 * TILES])
        weight = sb("weight", [P, 2 * TILES])
        tile_sums = sb("tile_sums", [P, 2 * TILES + 1])
        inv_den = sb("inv_den", [P, 2 * TILES])
        xw = sb("xw", [P, TILES, D])
        num_t = pair("num_t", [P, HALF])
        xf = sb("xf", [P, TILES, D])
        xft_hi, xft_lo = pair("xft_hi", [P, HALF], f32r), pair("xft_lo", [P, HALF], f32r)

        logit_t = sb("logit_t", [E, HALF])
        tanh_half = sb("tanh_half", [P, TILES, E])
        gate = sb("gate", [P, TILES, E])
        best = sb("best", [P, TILES, K])
        struck = sb("struck", [P, TILES, E])
        chosen = sb("chosen", [P, TILES, E])
        best_sum = sb("best_sum", [P, TILES])
        inv_best = sb("inv_best", [P, TILES])
        comb = sb("comb", [P, TILES, E])
        comb_hl = sb("comb_hl", [P, TILES, 2 * E], f32r)
        comb_t = pair("comb_t", [2 * E, HALF], f32r)

        silu = [sb(f"silu{i}", [P, HALF]) for i in range(3)]
        prod = [sb(f"prod{i}", [P, HALF]) for i in range(2)]
        hfull = [sb(f"hfull{i}", [P, HALF]) for i in range(3)]
        h_hi = [sb(f"h_hi{i}", [P, HALF], f32r) for i in range(4)]
        h_lo = [sb(f"h_lo{i}", [P, HALF], f32r) for i in range(4)]
        h_shared = sb("h_shared", [P, HALF], f32r)
        y_t = sb("y_t", [P, HALF])
        result = pair("result", [P, TILES, D])

        ps_gate = [pb(f"ps_gate{i}") for i in range(3)]
        ps_up = [pb("ps_up0"), pb("ps_up1")]
        ps_y = pb("ps_y")
        ps_a = pb("ps_a")
        ps_b = pb("ps_b")

        BANK = {(stage, h): {"a": ps_a, "b": ps_b}[bank]
                for stage, banks in BANKS.items() for h, bank in enumerate(banks)}

        def bank(stage, b, h):
            return ps_gate[0] if isinstance(b, int) and b == 0 and h == 1 else BANK[stage, h]

        names = """ident_in w1_in bias_in upto_in zeros_set gwt_in select_in shared_in gate_in up_in down_in
            consts_set w1t_ps w1t_split gw_squared gw_scaled gw_unit_set gwt_ps gwt_split gwt_zeroed
            select_set shared_hi shared_lo gu_hi_set gu_lo_set dn_hi_set dn_lo_set
            stats1_dve stats1_set scale1_pool scale1_set xn_set xnt_ps xnt_hi_set xnt_lo_set
            hid_ps hid_set score_ps score_row_set score_cols_ps score_dve top_set weight_pool
            weight_set sums_set den_ps inv_den_set xw_set xwt_ps num_set num_ps attended
            stats2_dve stats2_set scale2_pool scale2_set half_inv_set xf_set xft_ps xft_hi_set
            xft_lo_set logit_ps logit_set logit_cols_ps tanh_set route_dve comb_set comb_ps
            comb_t_set gate_ready up_ready comb_ready silu_set prod_set hfull_set h_hi_set
            h_lo_set shared_lo_set kept down_done y_set out_ps result_set""".split()
        s = {n: sem(n) for n in names}
        x_in_loaded = [sem("x_in_loaded0"), sem("x_in_loaded1")]
        x_raw_loaded = [sem("x_raw_loaded0"), sem("x_raw_loaded1")]
        stored = [sem("stored0"), sem("stored1")]

        block = ctx.enter_context(nc.Block())

        def half_no(b, h):
            return 2 * b + h

        def chunk_no(b, h, i):
            return STEPS * b + CHUNKS * h + i

        def wait(eng, name, value):
            if not isinstance(value, int) or value > 0:
                eng.wait_ge(s[name], value)

        def run(engine, step, stages, eng):
            offsets = {(name, h): off for n in STAGES[engine] for name, off, h in STAGES[engine][n]}

            def first(n):
                for name, b, h in FIRST_STAGES[n]:
                    if name in stages and offsets.get((name, h), 1) > b:
                        stages[name](b, h)

            def steps(b, begin, end, ahead):
                for n in range(begin, end):
                    def between():
                        if isinstance(b, int) and b == 0 and n + 1 < len(FIRST_STAGES):
                            first(n + 1)
                        for name, off, h in STAGES[engine].get(n, ()):
                            if off <= ahead and not (off < 0 and isinstance(b, int) and b == 0):
                                stages[name](b + off, h)
                    step(b, n // CHUNKS, n % CHUNKS, between)

            first(0)
            steps(0, 0, HEAD, AHEAD)
            with eng.Fori(0, B - AHEAD) as b:
                steps(b, HEAD, STEPS, AHEAD)
                steps(b + 1, 0, HEAD, AHEAD)
            for b in range(B - AHEAD, B):
                steps(b, HEAD, STEPS, B - 1 - b)
                if b + 1 < B:
                    steps(b + 1, 0, HEAD, B - 2 - b)

        def tile(t):
            return slice(t * P, (t + 1) * P)

        @block.sync
        def _(sp):
            def rows(src, b, h):
                return src[b, h * HALF:(h + 1) * HALF, :].rearrange("(t p) d -> p t d", p=P)

            sp.dma_start(x_in[0][:], rows(x, 0, 0)).then_inc(x_in_loaded[0], 16)
            sp.dma_start(x_in[1][:], rows(x, 0, 1)).then_inc(x_in_loaded[1], 16)
            sp.dma_start(gu_sb[:, 0:H], sw_gate).then_inc(s["shared_in"], 16)
            sp.dma_start(gu_sb[:, H:2 * H], sw_up).then_inc(s["shared_in"], 16)
            sp.dma_start(gu_sb[:, 2 * H:2 * H + E * H].rearrange("d (e h) -> d e h", e=E),
                         w_gate.rearrange("e d h -> d e h")).then_inc(s["gate_in"], 16)
            sp.dma_start(upto_sb[:], upto).then_inc(s["upto_in"], 16)
            sp.dma_start(gu_sb[:, 2 * H + E * H:GU].rearrange("d (e h) -> d e h", e=E),
                         w_up.rearrange("e d h -> d e h")).then_inc(s["up_in"], 16)
            sp.dma_start(select_f[:], pair_select).then_inc(s["select_in"], 16)
            sp.dma_start(x_raw[0][:], rows(x, 0, 0)).then_inc(x_raw_loaded[0], 16)
            sp.dma_start(dn_sb[:, D:].rearrange("p (c d) -> p c d", c=PAIRS),
                         w_down.rearrange("(c e) h d -> (e h) c d", c=PAIRS)).then_inc(s["down_in"], 16)
            sp.dma_start(dn_sb[0:H, 0:D], sw_down).then_inc(s["down_in"], 16)
            sp.dma_start(dn_sb[H:P, 0:D], sw_down).then_inc(s["down_in"], 16)
            sp.dma_start(x_raw[1][:], rows(x, 0, 1)).then_inc(x_raw_loaded[1], 16)

            def load_in(b):
                for h in range(2):
                    sp.wait_ge(s["xn_set"], half_no(b - 1, h) + 1)
                    sp.dma_start(x_in[h][:], rows(x, b, h)).then_inc(x_in_loaded[h], 16)

            def load_raw(b):
                for h in range(2):
                    sp.wait_ge(s["attended"], half_no(b - 1, h) + 1)
                    sp.dma_start(x_raw[h][:], rows(x, b, h)).then_inc(x_raw_loaded[h], 16)

            def store(b):
                for h in range(2):
                    sp.wait_ge(s["result_set"], half_no(b, h) + 2)
                    sp.dma_start(rows(out, b, h), result[h][:]).then_inc(stored[h], 16)

            load_in(1)
            with sp.Fori(0, B - AHEAD) as b:
                load_raw(b + 1)
                load_in(b + 2)
                store(b)
            load_raw(B - 1)
            store(B - 2)
            store(B - 1)
            for h in range(2):
                sp.wait_ge(stored[h], 16 * (B + 1))

        @block.scalar
        def _(act):
            act.dma_start(ident[:], identity).then_inc(s["ident_in"], 16)
            act.dma_start(w1_sb[:], w1).then_inc(s["w1_in"], 16)
            act.dma_start(b1_col[:], b1.rearrange("(p o) -> p o", o=1)).then_inc(s["bias_in"], 16)
            act.dma_start(w2_col[:], w2.rearrange("o p -> p o")).then_inc(s["bias_in"], 16)
            act.dma_start(b2_sb[:], b2.rearrange("(p o) -> p o", o=1)).then_inc(s["bias_in"], 16)
            act.dma_start(gw_sb[:], gate_w).then_inc(s["gwt_in"], 16)

            act.wait_ge(s["zeros_set"], 1)
            nc.scalar.activation(first_silu[:], zeros[0:1, 0:1], ACT.Silu)

            def shared_weights(b, h):
                act.wait_ge(s["shared_in"], 32)
                nc.scalar.copy(gu_hi[:, 0:2 * H], gu_sb[:, 0:2 * H]).then_inc(s["shared_hi"], 1)

            def gate_weights(b, h):
                act.wait_ge(s["gate_in"], 16)
                nc.scalar.copy(gu_hi[:, GATE], gu_sb[:, GATE]).then_inc(s["gu_hi_set"], 1)

            def up_weights(b, h):
                act.wait_ge(s["up_in"], 16)
                nc.scalar.copy(gu_hi[:, UP], gu_sb[:, UP]).then_inc(s["gu_hi_set"], 1)
                act.wait_ge(s["select_in"], 16)
                nc.scalar.copy(select[:], select_f[:]).then_inc(s["select_set"], 1)

            def down_weights(b, h):
                act.wait_ge(s["down_in"], 48)
                nc.scalar.copy(dn_hi[:], dn_sb[:]).then_inc(s["dn_hi_set"], 1)

            def norm1(b, h):
                n = half_no(b, h)
                act.wait_ge(s["scale1_set"], n + 1)
                for t in range(TILES):
                    last = nc.scalar.activation(xn[h][:, t, :], x_in[h][:, t, :], ACT.Identity,
                                                bias=shift1[h][:, t:t + 1], scale=rstd1[h][:, t:t + 1])
                last.then_inc(s["xn_set"], 1)

            def spread1(b, h):
                act.wait_ge(s["xnt_ps"], half_no(b, h) + 1)
                nc.scalar.copy(xnt_hi[h][:], bank("spread1", b, h)[:]).then_inc(s["xnt_hi_set"], 1)

            def hidden(b, h):
                act.wait_ge(s["hid_ps"], half_no(b, h) + 1)
                if isinstance(b, int) and b == 0 and h == 0:
                    act.wait_ge(s["bias_in"], 16 * 3)
                nc.scalar.activation(hid[h][:], bank("hidden", b, h)[:], ACT.Tanh, bias=b1_col[:, 0:1]).then_inc(s["hid_set"], 1)

            def weigh(b, h):
                n = half_no(b, h)
                act.wait_ge(s["weight_set"], b + 1)
                wait(act, "xwt_ps", n)
                for t in range(TILES):
                    last = nc.scalar.activation(xw[:, t, :], xn[h][:, t, :], ACT.Copy,
                                                scale=weight[:, h * TILES + t:h * TILES + t + 1])
                last.then_inc(s["xw_set"], 1)

            def norm2(b, h):
                n = half_no(b, h)
                act.wait_ge(s["scale2_set"], n + 1)
                wait(act, "xft_ps", n)
                for t in range(TILES):
                    last = nc.scalar.activation(xf[:, t, :], x_att[h][:, t, :], ACT.Identity,
                                                bias=shift2[h][:, t:t + 1], scale=rstd2[h][:, t:t + 1])
                last.then_inc(s["xf_set"], 1)

            def spread2(b, h):
                act.wait_ge(s["xft_ps"], half_no(b, h) + 1)
                nc.scalar.copy(xft_hi[h][:], BANK["spread2", h][:]).then_inc(s["xft_hi_set"], 1)

            def logits(b, h):
                act.wait_ge(s["logit_ps"], half_no(b, h) + 1)
                nc.scalar.copy(logit_t[:], BANK["logits", h][0:E, :]).then_inc(s["logit_set"], 1)

            def gates(b, h):
                n = half_no(b, h)
                act.wait_ge(s["logit_cols_ps"], n + 1)
                act.wait_ge(s["half_inv_set"], n + 1)
                wait(act, "comb_set", n)
                for t in range(TILES):
                    last = nc.scalar.activation(tanh_half[:, t, :], BANK["gates", h][:, t * E:(t + 1) * E],
                                                ACT.Tanh, scale=half_inv[h][:, t:t + 1])
                last.then_inc(s["tanh_set"], 1)

            def route(b, h):
                act.wait_ge(s["comb_ps"], half_no(b, h) + 1)
                nc.scalar.copy(comb_t[h][:], BANK["route", h][0:2 * E, :]).then_inc(s["comb_t_set"], 1)

            def hidden_high(b, h, i):
                if i == 0:
                    act.wait_ge(s["prod_set"], chunk_no(b, h, 1))
                    last = nc.scalar.copy(h_shared[0:H, :], hfull[(CHUNKS * h) % 3][0:H, :])
                else:
                    act.wait_ge(s["hfull_set"], PAIRS * half_no(b, h) + i)
                    last = nc.scalar.copy(h_hi[i % 4][:], hfull[(CHUNKS * h + i) % 3][:])
                last.then_inc(s["h_hi_set"], 1)

            def before(b, h, i):
                return (b, h, i - 1) if i else ((b, 0, CHUNKS - 1) if h else (b - 1, 1, CHUNKS - 1))

            def score_stage(b, h):
                act.wait_ge(s["score_ps"], half_no(b, h) + 1)
                if h == 0:
                    wait(act, "score_cols_ps", b)
                nc.scalar.activation(score_row[h][:], bank("score", b, h)[0:1, :], ACT.Identity,
                                     bias=b2_sb[0:1, 0:1]).then_inc(s["score_row_set"], 1)

            def step(b, h, i, between):
                c = chunk_no(b, h, i)
                act.wait_ge(s["gate_ready"], c + 1)
                wait(act, "prod_set", c - 2)
                rows = slice(0, H if i == 0 else P)
                buf = (CHUNKS * h + i) % 3
                nc.scalar.activation(silu[buf][rows, :], ps_gate[buf][rows, :], ACT.Silu).then_inc(s["silu_set"], 1)
                if not (isinstance(c, int) and c == 0):
                    hidden_high(*before(b, h, i))
                between()

            def collect(b, h):
                act.wait_ge(s["down_done"], chunk_no(b, h, CHUNKS))
                nc.scalar.copy(y_t[:], ps_y[:]).then_inc(s["y_set"], 1)

            run("act", step, {
                       "shared_weights": shared_weights, "gate_weights": gate_weights, "up_weights": up_weights,
                       "down_weights": down_weights, "score": score_stage, "norm1": norm1, "spread1": spread1, "hidden": hidden,
                       "weigh": weigh, "norm2": norm2, "spread2": spread2, "logits": logits, "gates": gates,
                       "route": route, "collect": collect}, act)
            hidden_high(B - 1, 1, CHUNKS - 1)
            collect(B - 1, 1)

        @block.gpsimd
        def _(pool):
            nc.gpsimd.memset(euler[:], 2.718281828459045).then_inc(s["consts_set"], 1)
            nc.gpsimd.memset(minus_half[:], -0.5).then_inc(s["consts_set"], 1)
            nc.gpsimd.memset(ones[:], 1.0).then_inc(s["consts_set"], 1)
            nc.gpsimd.memset(zeros[:], 0.0).then_inc(s["zeros_set"], 1)
            nc.gpsimd.memset(tile_sums[:, 0:1], 0.0).then_inc(s["consts_set"], 1)
            nc.gpsimd.memset(gwt[:], 0.0).then_inc(s["gwt_zeroed"], 1)
            pool.wait_ge(s["consts_set"], 4)
            pool.wait_ge(s["zeros_set"], 1)

            def router_weights(b, h):
                pool.wait_ge(s["gw_squared"], 2)
                nc.gpsimd.tensor_tensor(gw_inv[:], gw_n2[:], minus_half[0:E, 0:1], ALU.pow).then_inc(s["gw_scaled"], 1)

            def stats1(b, h):
                n = half_no(b, h)
                pool.wait_ge(s["stats1_set"], n + 1)
                nc.gpsimd.tensor_tensor(rstd1[h][:], var_eps1[h][:], minus_half[:], ALU.pow).then_inc(s["scale1_pool"], 1)
                pool.wait_ge(s["scale1_pool"], n + 1)
                nc.gpsimd.tensor_tensor(shift1[h][:], neg_mean1[h][:], rstd1[h][:], ALU.mult).then_inc(s["scale1_set"], 1)

            def softmax(b, h):
                pool.wait_ge(s["top_set"], b + 1)
                nc.gpsimd.tensor_tensor(own_score[:], score[:], zeros[:, 0:2 * TILES], ALU.add)
                nc.gpsimd.partition_all_reduce(top_all[:], top[:], P, bass.bass_isa.ReduceOp.max).then_inc(s["weight_pool"], 1)

            def powers(b, h):
                pool.wait_ge(s["weight_pool"], 2 * b + 1)
                nc.gpsimd.tensor_tensor(below[:], own_score[:], top_all[:].broadcast_to([P, 2 * TILES]),
                                        ALU.subtract).then_inc(s["weight_pool"], 1)
                pool.wait_ge(s["weight_pool"], 2 * b + 2)
                wait(pool, "xw_set", 2 * b)
                nc.gpsimd.tensor_tensor(weight[:], euler[:], below[:], ALU.pow).then_inc(s["weight_set"], 1)

            def scale2(b, h):
                n = half_no(b, h)
                pool.wait_ge(s["stats2_set"], n + 1)
                nc.gpsimd.tensor_tensor(rstd2[h][:], var_eps2[h][:], minus_half[:], ALU.pow).then_inc(s["scale2_pool"], 1)
                pool.wait_ge(s["scale2_pool"], 3 * n + 1)
                nc.gpsimd.tensor_tensor(shift2[h][:], neg_mean2[h][:], rstd2[h][:], ALU.mult).then_inc(s["scale2_set"], 1)

            def norms(b, h):
                n = half_no(b, h)
                pool.wait_ge(s["scale2_pool"], 3 * n + 1)
                nc.gpsimd.tensor_tensor(xf_norm[h][:], var512[h][:], rstd2[h][:], ALU.mult).then_inc(s["scale2_pool"], 1)
                pool.wait_ge(s["scale2_pool"], 3 * n + 2)
                nc.gpsimd.tensor_tensor(xf_norm2[h][:], xf_norm[h][:], rstd2[h][:], ALU.mult)
                pool.drain()
                nc.gpsimd.tensor_scalar(xf_norm3[h][:], xf_norm2[h][:], 4 * NORM_EPS ** 2, None,
                                        ALU.max).then_inc(s["scale2_pool"], 1)
                pool.wait_ge(s["scale2_pool"], 3 * n + 3)
                nc.gpsimd.tensor_tensor(half_inv[h][:], xf_norm3[h][:], minus_half[:], ALU.pow).then_inc(s["half_inv_set"], 1)

            def keep(b, h):
                pool.wait_ge(s["attended"], half_no(b, h) + 1)
                pool.wait_ge(stored[h], 16 * b + 16)
                nc.gpsimd.tensor_tensor(result[h][:].rearrange("p t d -> p (t d)"), zeros[:],
                                        x_att[h][:].rearrange("p t d -> p (t d)"), ALU.add).then_inc(s["kept"], 1)

            def hidden_low(b, h, i):
                if i == 0:
                    return
                pool.wait_ge(s["h_hi_set"], chunk_no(b, h, i) + 1)
                nc.gpsimd.tensor_tensor(h_lo[i % 4][:], hfull[(CHUNKS * h + i) % 3][:], word(h_hi[i % 4][:]),
                                        ALU.subtract).then_inc(s["h_lo_set"], 1)

            def step(b, h, i, between):
                if i:
                    hidden_low(b, h, i - 1)
                elif not (isinstance(b, int) and b == 0 and h == 0):
                    hidden_low(*((b, 0) if h else (b - 1, 1)), CHUNKS - 1)
                between()

            run("pool", step, {"router_weights": router_weights, "stats1": stats1, "softmax": softmax, "powers": powers,
                                      "scale2": scale2, "norms": norms, "keep": keep}, pool)
            hidden_low(B - 1, 1, CHUNKS - 1)

        @block.vector
        def _(dve):
            def low(out_, whole, hi, name):
                return nc.vector.tensor_tensor(out_, whole, word(hi), ALU.subtract).then_inc(s[name], 1)

            def hidden_weights(b, h):
                dve.wait_ge(s["w1t_ps"], 1)
                nc.vector.tensor_copy(w1t[:], ps_up[0][:, 0:P]).then_inc(s["w1t_split"], 1)
                dve.wait_ge(s["w1t_split"], 1)
                nc.vector.tensor_copy(w1t_hi[:], w1t[:]).then_inc(s["w1t_split"], 1)
                dve.wait_ge(s["w1t_split"], 2)
                low(w1t_lo[:], w1t[:], w1t_hi[:], "w1t_split")

            def router_weights(b, h):
                dve.wait_ge(s["gwt_in"], 16)
                nc.vector.scalar_tensor_tensor(out=gw_sq[:], in0=gw_sb[:], scalar=1.0, in1=gw_sb[:], op0=ALU.mult,
                                               op1=ALU.mult).then_inc(s["gw_squared"], 1)
                dve.wait_ge(s["gw_squared"], 1)
                nc.vector.tensor_reduce(gw_inv[:], gw_sq[:], AX.X, ALU.add).then_inc(s["gw_unit_set"], 1)
                dve.wait_ge(s["gw_unit_set"], 1)
                nc.vector.tensor_scalar(gw_n2[:], gw_inv[:], NORM_EPS ** 2, None, ALU.max).then_inc(s["gw_squared"], 1)
                dve.wait_ge(s["gw_scaled"], 1)
                nc.vector.tensor_scalar(gw_unit[:], gw_sb[:], gw_inv[:, 0:1], None, ALU.mult).then_inc(s["gw_unit_set"], 1)
                dve.wait_ge(s["gwt_zeroed"], 1)
                dve.wait_ge(s["gwt_ps"], 1)
                nc.vector.tensor_copy(gwt[:, 0:E], ps_up[1][:, 0:E]).then_inc(s["gwt_split"], 1)
                dve.wait_ge(s["gwt_split"], 1)
                nc.vector.tensor_copy(gwt_hi[:], gwt[:]).then_inc(s["gwt_split"], 1)
                dve.wait_ge(s["gwt_split"], 2)
                low(gwt_lo[:], gwt[:], gwt_hi[:], "gwt_split")

            def shared_weights(b, h):
                dve.wait_ge(s["shared_hi"], 1)
                low(gu_lo[:, 0:2 * H], gu_sb[:, 0:2 * H], gu_hi[:, 0:2 * H], "shared_lo")

            def gate_low(b, h):
                dve.wait_ge(s["gu_hi_set"], 1)
                low(gu_lo[:, GATE], gu_sb[:, GATE], gu_hi[:, GATE], "gu_lo_set")

            def up_low(b, h):
                dve.wait_ge(s["gu_hi_set"], 2)
                low(gu_lo[:, UP], gu_sb[:, UP], gu_hi[:, UP], "gu_lo_set")

            def down_low(b, h):
                dve.wait_ge(s["dn_hi_set"], 1)
                low(dn_lo[:], dn_sb[:], dn_hi[:], "dn_lo_set")

            def moments(src, bn, mv, chain, n):
                for t in range(TILES):
                    last = nc.vector.bn_stats(bn[:, t, :], src[:, t, :])
                dve.drain()
                for t in range(TILES):
                    last = nc.vector.bn_aggr(mv[:, t, :], bn[:, t, :])
                last.then_inc(s[chain], 1)
                dve.wait_ge(s[chain], n + 1)

            def stats1(b, h):
                n = half_no(b, h)
                dve.wait_ge(x_in_loaded[h], 16 * b + 16)
                wait(dve, "xn_set", n - 1)
                moments(x_in[h], bn1[h], mv1[h], "stats1_dve", n)
                nc.vector.tensor_scalar(neg_mean1[h][:], mv1[h][:, :, 0], -1.0, None, ALU.mult)
                nc.vector.tensor_scalar(var_eps1[h][:], mv1[h][:, :, 1], EPS, None, ALU.add).then_inc(s["stats1_set"], 1)

            def spread1(b, h):
                dve.wait_ge(s["xnt_hi_set"], half_no(b, h) + 1)
                low(xnt_lo[h][:], bank("spread1", b, h)[:], xnt_hi[h][:], "xnt_lo_set")

            def softmax(b, h):
                dve.wait_ge(s["score_cols_ps"], b + 1)
                wait(dve, "weight_set", b)
                nc.vector.tensor_copy(score[:], BANK["softmax", 0][:, 0:2 * TILES]).then_inc(s["score_dve"], 1)
                dve.wait_ge(s["score_dve"], b + 1)
                nc.vector.tensor_reduce(top[:], score[:], AX.X, ALU.max).then_inc(s["top_set"], 1)

            def sums(b, h):
                dve.wait_ge(s["weight_set"], b + 1)
                nc.vector.tensor_tensor_scan(tile_sums[:, 1:2 * TILES + 1], weight[:], zeros[:, 0:2 * TILES],
                                             0.0, ALU.add, ALU.add).then_inc(s["sums_set"], 1)

            def denominator(b, h):
                dve.wait_ge(s["den_ps"], b + 1)
                nc.vector.reciprocal(inv_den[:], BANK["denominator", 0][:, 0:2 * TILES]).then_inc(s["inv_den_set"], 1)

            def scan(b, h):
                n = half_no(b, h)
                dve.wait_ge(s["xwt_ps"], n + 1)
                if h == 1:
                    dve.wait_ge(s["num_set"], n)
                wait(dve, "num_ps", n - 1)
                start = num_t[0][:, HALF - 1:HALF] if h else 0.0
                nc.vector.tensor_tensor_scan(num_t[h][:], zeros[:], BANK["scan", h][:], start, ALU.add,
                                             ALU.add).then_inc(s["num_set"], 1)

            def attend(b, h):
                n = half_no(b, h)
                dve.wait_ge(s["num_ps"], n + 1)
                dve.wait_ge(s["inv_den_set"], b + 1)
                dve.wait_ge(x_raw_loaded[h], 16 * b + 16)
                wait(dve, "kept", half_no(b - 1, h) + 1)
                for t in range(TILES):
                    col = h * TILES + t
                    last = nc.vector.scalar_tensor_tensor(
                        out=x_att[h][:, t, :], in0=BANK["attend", h][:, tile(t)], scalar=inv_den[:, col:col + 1],
                        in1=x_raw[h][:, t, :], op0=ALU.mult, op1=ALU.add)
                last.then_inc(s["attended"], 1)

            def stats2(b, h):
                n = half_no(b, h)
                dve.wait_ge(s["attended"], n + 1)
                moments(x_att[h], bn2[h], mv2[h], "stats2_dve", n)
                nc.vector.tensor_scalar(neg_mean2[h][:], mv2[h][:, :, 0], -1.0, None, ALU.mult)
                nc.vector.tensor_scalar(var512[h][:], mv2[h][:, :, 1], 4.0 * D, None, ALU.mult)
                nc.vector.tensor_scalar(var_eps2[h][:], mv2[h][:, :, 1], EPS, None, ALU.add).then_inc(s["stats2_set"], 1)

            def spread2(b, h):
                dve.wait_ge(s["xft_hi_set"], half_no(b, h) + 1)
                low(xft_lo[h][:], BANK["spread2", h][:], xft_hi[h][:], "xft_lo_set")

            def choose(b, h):
                dve.wait_ge(s["tanh_set"], half_no(b, h) + 1)
                nc.vector.tensor_scalar(gate[:], tanh_half[:], 0.5, 0.5, ALU.mult, ALU.add)
                dve.drain()
                for t in range(TILES):
                    nc.vector.max(best[:, t, :], gate[:, t, :])
                dve.drain()
                for t in range(TILES):
                    last = nc.vector.match_replace(struck[:, t, :], best[:, t, :], gate[:, t, :], -1.0)
                last.then_inc(s["route_dve"], 1)

            def share(b, h):
                n = half_no(b, h)
                dve.wait_ge(s["route_dve"], 4 * n + 1)
                nc.vector.scalar_tensor_tensor(out=chosen[:], in0=struck[:], scalar=0.0, in1=gate[:],
                                               op0=ALU.is_lt, op1=ALU.mult)
                nc.vector.tensor_reduce(best_sum[:], best[:], AX.X, ALU.add).then_inc(s["route_dve"], 1)
                dve.wait_ge(s["route_dve"], 4 * n + 2)
                nc.vector.reciprocal(inv_best[:], best_sum[:]).then_inc(s["route_dve"], 1)
                dve.wait_ge(s["route_dve"], 4 * n + 3)
                scale = inv_best[:].unsqueeze(2).broadcast_to([P, TILES, E])
                nc.vector.tensor_tensor(comb[:], chosen[:], scale, ALU.mult)
                wait(dve, "comb_ps", n)
                nc.vector.tensor_tensor(comb_hl[:, :, 0:E], chosen[:], scale, ALU.mult).then_inc(s["route_dve"], 1)
                dve.wait_ge(s["route_dve"], 4 * n + 4)
                low(comb_hl[:, :, E:2 * E], comb[:], comb_hl[:, :, 0:E], "comb_set")

            def step(b, h, i, between):
                chunk(b, h, i)
                between()

            def chunk(b, h, i):
                c = chunk_no(b, h, i)
                n = half_no(b, h)
                buf = (CHUNKS * h + i) % 3
                dve.wait_ge(s["silu_set"], c + 1)
                if i == 0:
                    wait(dve, "h_lo_set", PAIRS * n - 2)
                    nc.vector.tensor_tensor(hfull[buf][0:H, :], silu[buf][0:H, :], ps_gate[buf][H:P, :],
                                            ALU.mult).then_inc(s["prod_set"], 1)
                    return
                up = (CHUNKS * h + i) % 2
                dve.wait_ge(s["up_ready"], PAIRS * n + i)
                nc.vector.tensor_tensor(prod[up][:], silu[buf][:], ps_up[up][:], ALU.mult).then_inc(s["prod_set"], 1)
                dve.wait_ge(s["comb_ready"], PAIRS * n + i)
                dve.wait_ge(s["prod_set"], c + 1)
                if i == 3:
                    dve.wait_ge(s["shared_lo_set"], n + 1)
                else:
                    wait(dve, "h_lo_set", PAIRS * n + {1: -1, 2: 0}.get(i, i - 3))
                nc.vector.tensor_tensor(hfull[buf][:], prod[up][:], ps_gate[buf][:], ALU.mult).then_inc(s["hfull_set"], 1)
                if i == 1:
                    dve.wait_ge(s["h_hi_set"], chunk_no(b, h, 1))
                    low(h_shared[H:P, :], hfull[(CHUNKS * h) % 3][0:H, :], h_shared[0:H, :], "shared_lo_set")

            def out_stage(b, h):
                dve.wait_ge(s["out_ps"], half_no(b, h) + 1)
                dve.wait_ge(s["kept"], half_no(b, h) + 1)
                flat = result[h][:].rearrange("p t d -> p (t d)")
                nc.vector.tensor_tensor(flat, BANK["out", h][:], flat, ALU.add).then_inc(s["result_set"], 1)

            nc.vector.memset(started[:, 0:1], 0.0).then_inc(stored[0], 16)
            nc.vector.memset(started[:, 1:2], 0.0).then_inc(stored[1], 16)
            nc.vector.memset(started[:, 2:3], 0.0).then_inc(s["result_set"], 1)
            run("dve", step, {
                       "hidden_weights": hidden_weights, "router_weights": router_weights,
                       "shared_weights": shared_weights,
                       "gate_low": gate_low, "up_low": up_low, "down_low": down_low,
                       "stats1": stats1, "spread1": spread1, "softmax": softmax, "sums": sums,
                       "denominator": denominator, "scan": scan, "attend": attend, "stats2": stats2,
                       "spread2": spread2, "choose": choose, "share": share,
                       "out": out_stage}, dve)
            out_stage(B - 1, 1)

        @block.tensor
        def _(pe):
            mm = nc.tensor.matmul

            def split_product(out_, w_hi, w_lo, m_hi, m_lo, start=True, stop=True):
                mm(out_, w_hi, m_lo, start=start, stop=False)
                mm(out_, w_lo, m_hi, start=False, stop=False)
                return mm(out_, w_hi, m_hi, start=False, stop=stop)

            def transposes(out_, src):
                for t in range(TILES):
                    last = nc.tensor.transpose(out_[:, tile(t)], src(t), ident[:])
                return last

            def turn(t, out_, src, eye):
                if t == 0:
                    return mm(out_, src, eye, start=True, stop=True)
                return nc.tensor.transpose(out_, src, eye)

            def is_int(b, value):
                return isinstance(b, int) and b == value

            def hidden_weights(b, h):
                pe.wait_ge(s["ident_in"], 16)
                pe.wait_ge(s["w1_in"], 16)
                nc.tensor.transpose(ps_up[0][:, 0:P], w1_sb[:], ident[:]).then_inc(s["w1t_ps"], 1)

            def router_weights(b, h):
                pe.wait_ge(s["gw_unit_set"], 2)
                nc.tensor.transpose(ps_up[1][:, 0:E], gw_unit[:], ident[0:E, 0:E]).then_inc(s["gwt_ps"], 1)

            def spread1(b, h):
                if h == 0:
                    wait(pe, "attended", half_no(b - 1, 1) + 1)
                if h == 1 and not is_int(b, 0):
                    wait(pe, "logit_set", half_no(b - 1, 1) + 1)
                pe.wait_ge(s["xn_set"], half_no(b, h) + 1)
                transposes(bank("spread1", b, h), lambda t: xn[h][:, t, :]).then_inc(s["xnt_ps"], 1)

            def hidden(b, h):
                pe.wait_ge(s["xnt_lo_set"], half_no(b, h) + 1)
                if is_int(b, 0) and h == 0:
                    pe.wait_ge(s["w1t_split"], 3)
                split_product(bank("hidden", b, h)[:], w1t_hi[:], w1t_lo[:], xnt_hi[h][:],
                              xnt_lo[h][:]).then_inc(s["hid_ps"], 1)

            def score_stage(b, h):
                if h == 0:
                    wait(pe, "tanh_set", half_no(b - 1, 0) + 1)
                pe.wait_ge(s["hid_set"], half_no(b, h) + 1)
                if is_int(b, 0) and h == 0:
                    pe.wait_ge(s["bias_in"], 16 * 3)
                mm(bank("score", b, h)[0:1, :], w2_col[:], hid[h][:], start=True, stop=True).then_inc(s["score_ps"], 1)

            def softmax(b, h):
                pe.wait_ge(s["score_row_set"], 2 * b + 2)
                for t in range(2 * TILES):
                    last = turn(t, BANK["softmax", 0][:, t:t + 1], score_row[t // TILES][:, tile(t % TILES)],
                                ident[0:1, 0:1])
                last.then_inc(s["score_cols_ps"], 1)

            def scan(b, h):
                if h == 1:
                    pe.wait_ge(s["attended"], half_no(b, 0) + 1)
                pe.wait_ge(s["xw_set"], half_no(b, h) + 1)
                if h == 0:
                    pe.wait_ge(s["inv_den_set"], b + 1)
                transposes(BANK["scan", h], lambda t: xw[:, t, :]).then_inc(s["xwt_ps"], 1)

            def denominator(b, h):
                wait(pe, "comb_t_set", half_no(b - 1, 1) + 1)
                pe.wait_ge(s["sums_set"], b + 1)
                if is_int(b, 0):
                    pe.wait_ge(s["upto_in"], 16)
                    pe.wait_ge(s["consts_set"], 4)
                den = BANK["denominator", 0][:, 0:2 * TILES]
                mm(den, ones[:], tile_sums[:, 0:2 * TILES], start=True, stop=False)
                mm(den, upto_sb[:], weight[:], start=False, stop=True).then_inc(s["den_ps"], 1)

            def attend(b, h):
                pe.wait_ge(s["num_set"], half_no(b, h) + 1)
                transposes(BANK["attend", h], lambda t: num_t[h][:, tile(t)]).then_inc(s["num_ps"], 1)

            def spread2(b, h):
                if h == 0:
                    wait(pe, "result_set", half_no(b - 1, 0) + 2)
                if h == 1 and not (isinstance(b, int) and b + 1 >= B):
                    pe.wait_ge(s["hid_set"], half_no(b + 1, 0) + 1)
                pe.wait_ge(s["xf_set"], half_no(b, h) + 1)
                transposes(BANK["spread2", h], lambda t: xf[:, t, :]).then_inc(s["xft_ps"], 1)

            def logits(b, h):
                pe.wait_ge(s["xft_lo_set"], half_no(b, h) + 1)
                if is_int(b, 0) and h == 0:
                    pe.wait_ge(s["gwt_split"], 3)
                split_product(BANK["logits", h][:], gwt_hi[:], gwt_lo[:], xft_hi[h][:],
                              xft_lo[h][:]).then_inc(s["logit_ps"], 1)

            def gates(b, h):
                if h == 1:
                    pe.wait_ge(s["comb_t_set"], half_no(b, 0) + 1)
                pe.wait_ge(s["logit_set"], half_no(b, h) + 1)
                for t in range(TILES):
                    last = turn(t, BANK["gates", h][:, t * E:(t + 1) * E], logit_t[:, tile(t)], ident[0:E, 0:E])
                last.then_inc(s["logit_cols_ps"], 1)

            def route(b, h):
                if h == 0 and not (isinstance(b, int) and b + 1 >= B):
                    pe.wait_ge(s["score_row_set"], half_no(b + 1, 0) + 1)
                if h == 1:
                    wait(pe, "result_set", half_no(b - 1, 1) + 2)
                pe.wait_ge(s["comb_set"], half_no(b, h) + 1)
                for t in range(TILES):
                    last = nc.tensor.transpose(BANK["route", h][0:2 * E, tile(t)], word(comb_hl[:, t, :]), ident[:])
                last.then_inc(s["comb_ps"], 1)

            def out_stage(b, h):
                if h == 1 and not (isinstance(b, int) and b + 1 >= B):
                    pe.wait_ge(s["tanh_set"], half_no(b + 1, 1) + 1)
                pe.wait_ge(s["y_set"], half_no(b, h) + 1)
                transposes(BANK["out", h], lambda t: y_t[:, tile(t)]).then_inc(s["out_ps"], 1)

            def down(b, h, i):
                n = half_no(b, h)
                cols = slice(i * D, (i + 1) * D)
                pe.wait_ge(s["h_hi_set"], chunk_no(b, h, i) + 1)
                if i == 0:
                    pe.wait_ge(s["shared_lo_set"], n + 1)
                    wait(pe, "y_set", n)
                    if is_int(b, 0) and h == 0:
                        pe.wait_ge(s["dn_lo_set"], 1)
                    mm(ps_y[:], dn_lo[:, cols], h_shared[:], start=True, stop=False)
                    last = mm(ps_y[:], dn_hi[:, cols], h_shared[:], start=False, stop=False)
                else:
                    pe.wait_ge(s["h_lo_set"], PAIRS * n + i)
                    last = split_product(ps_y[:], dn_hi[:, cols], dn_lo[:, cols], h_hi[i % 4][:], h_lo[i % 4][:],
                                         start=False, stop=i == CHUNKS - 1)
                last.then_inc(s["down_done"], 1)

            def step(b, h, i, between):
                c = chunk_no(b, h, i)
                n = half_no(b, h)
                buf = (CHUNKS * h + i) % 3
                up = (CHUNKS * h + i) % 2
                if i == 0:
                    pe.wait_ge(s["xft_lo_set"], n + 1)
                    if is_int(b, 0) and h == 0:
                        pe.wait_ge(s["shared_lo"], 1)
                if i == 1 and is_int(b, 0) and h == 0:
                    pe.wait_ge(s["gu_lo_set"], 2)
                    pe.wait_ge(s["select_set"], 1)
                if i == 3:
                    pe.wait_ge(s["prod_set"], c - 2)
                else:
                    wait(pe, "hfull_set", PAIRS * n + {0: -2, 1: -1, 2: 0}.get(i, i - 3))

                def from_x(bank, first):
                    cols = slice(first, first + P)
                    return split_product(bank[:], gu_hi[:, cols], gu_lo[:, cols], xft_hi[h][:], xft_lo[h][:])

                if i == 0:
                    from_x(ps_gate[buf], 0).then_inc(s["gate_ready"], 1)
                else:
                    from_x(ps_gate[buf], GATE.start + (i - 1) * P).then_inc(s["gate_ready"], 1)
                    wait(pe, "prod_set", c - 1)
                    from_x(ps_up[up], UP.start + (i - 1) * P).then_inc(s["up_ready"], 1)
                between()
                if i >= LAG:
                    down(b, h, i - LAG)
                elif h:
                    down(b, 0, CHUNKS + i - LAG)
                elif not is_int(b, 0):
                    down(b - 1, 1, CHUNKS + i - LAG)
                if i:
                    if i == 1:
                        pe.wait_ge(s["comb_t_set"], n + 1)
                    pe.wait_ge(s["silu_set"], c + 1)
                    mm(ps_gate[buf][:], select[:, (i - 1) * P:i * P], comb_t[h][:], start=True,
                       stop=True).then_inc(s["comb_ready"], 1)

            run("pe", step, {
                       "hidden_weights": hidden_weights, "router_weights": router_weights,
                       "spread1": spread1, "hidden": hidden, "score": score_stage,
                       "softmax": softmax, "scan": scan, "denominator": denominator, "attend": attend,
                       "spread2": spread2, "logits": logits, "gates": gates, "route": route, "out": out_stage},
                pe)
            for i in range(CHUNKS - LAG, CHUNKS):
                down(B - 1, 1, i)
            out_stage(B - 1, 1)


_INS = ["L0_attn_x", "L0_attn_W1", "L0_attn_b1_", "L0_attn_W2", "L0_attn_b2_", "L0_ffn_gate_w", "L0_ffn_w_gate",
        "L0_ffn_w_up", "L0_ffn_w_down", "L0_ffn_sw_gate", "L0_ffn_sw_up", "L0_ffn_sw_down"]


def kernel(**inputs):
    import numpy as np
    import concourse.bacc as bacc
    from concourse.bass_utils import run_bass_kernel_spmd

    arrays = {f"in_{name}": np.ascontiguousarray(inputs[name]) for name in _INS}
    arrays["identity"] = np.eye(P, dtype=np.float32)
    arrays["pair_select"] = np.tile(np.kron(np.eye(E, dtype=np.float32), np.ones((1, H), np.float32)), (2, 1))
    arrays["upto"] = np.triu(np.ones((P, P), np.float32))
    nc = bacc.Bacc("TRN2", target_bir_lowering=False, num_devices=1)
    args = [nc.dram_tensor(name, a.shape, mybir.dt.from_np(a.dtype), kind="ExternalInput").ap()
            for name, a in arrays.items()]
    result = nc.dram_tensor("out_dram", (B, T, D), mybir.dt.float32, kind="ExternalOutput").ap()
    attention_moe_kernel(nc, *args, result)
    r = run_bass_kernel_spmd(nc, [arrays], core_ids=[0])
    return r.results[0]["out_dram"]
```
